# Optimizing a Trainium2 kernel written in Bass

```python
import numpy as np
import jax
import jax.numpy as jnp

def _softmax(x, axis=-1):
    return jax.nn.softmax(x, axis=axis)

def _gelu(x):
    return jax.nn.gelu(x, approximate=True)

def _silu(x):
    return jax.nn.silu(x)

def _sigmoid(x):
    return jax.nn.sigmoid(x)

def _layernorm(x, axis=-1, eps=1e-05):
    m = jnp.mean(x, axis=axis, keepdims=True)
    v = jnp.var(x, axis=axis, keepdims=True)
    return (x - m) / jnp.sqrt(v + eps)

def _scatter_add(tgt, idx, src, axis=0):
    return tgt.at[idx].add(src)

def _segment_sum(src, seg, n):
    return jax.ops.segment_sum(src, seg, n)
kernel_name = 'mk_hybrid_d1_jaxref_r8_543819'

def setup_inputs(seed: int=0):
    np.random.seed(seed)
    _w = jnp.asarray

    def _L0_attn_a_setup():
        import jax, jax.numpy as jnp
        import numpy as np
        H = 512
        D = H // 4
        key = jax.random.key(seed)
        k1, k2, k3, k4, k5 = jax.random.split(key, 5)
        x = jax.random.normal(k1, (4, 512, H), dtype=jnp.float32)
        s_in = 1.0 / np.sqrt(H)
        Wqkv = jax.random.normal(k2, (H, 3 * D), dtype=jnp.float32) * s_in
        bqkv = jax.random.normal(k3, (3 * D,), dtype=jnp.float32) * 0.01
        Wo = jax.random.normal(k4, (D, H), dtype=jnp.float32) * (1.0 / np.sqrt(D))
        bo = jax.random.normal(k5, (H,), dtype=jnp.float32) * 0.01
        return {'x': x, 'Wqkv': Wqkv, 'bqkv': bqkv, 'Wo': Wo, 'bo': bo}
    _L0_attn_a_in = _L0_attn_a_setup()

    def _L0_attn_b_setup():
        import jax, jax.numpy as jnp
        import numpy as np
        B, S, D = (2, 256, 512)
        H = 32
        HD = D // H
        THETA = 10000.0

        def _rope_cos_sin(seq_len, head_dim, theta=THETA):
            inv = 1.0 / theta ** (np.arange(0, head_dim, 2)[:head_dim // 2].astype(np.float32) / head_dim)
            t = np.arange(seq_len)
            f = np.outer(t, inv).astype(np.float32)
            return (jnp.asarray(np.cos(f)), jnp.asarray(np.sin(f)))

        def _apply_rotary(x, cos, sin):
            xr = x.astype(jnp.float32).reshape(*x.shape[:-1], HD // 2, 2)
            x0, x1 = (xr[..., 0], xr[..., 1])
            c = cos[None, :, None, :]
            s = sin[None, :, None, :]
            o0 = x0 * c - x1 * s
            o1 = x0 * s + x1 * c
            return jnp.stack((o0, o1), axis=-1).reshape(*x.shape[:-1], HD)
        key = jax.random.key(seed)
        ks = jax.random.split(key, 5)
        std = 0.02
        return {'x': jax.random.normal(ks[0], (B, S, D), dtype=jnp.float32), 'wq': jax.random.normal(ks[1], (D, D), dtype=jnp.float32) * std, 'wk': jax.random.normal(ks[2], (D, D), dtype=jnp.float32) * std, 'wv': jax.random.normal(ks[3], (D, D), dtype=jnp.float32) * std, 'wo': jax.random.normal(ks[4], (D, D), dtype=jnp.float32) * std}
    _L0_attn_b_in = _L0_attn_b_setup()

    def _L0_ffn_setup():
        import jax, jax.numpy as jnp
        import numpy as np
        NIBBLE_MASK = 15

        def _dequant_weight(qweight, scale, zero):
            q = qweight.astype(jnp.int32)
            low = q & NIBBLE_MASK
            high = q >> 4 & NIBBLE_MASK
            OC = q.shape[0]
            w_int = jnp.stack([high, low], axis=-1).reshape(OC, -1)
            return (w_int.astype(scale.dtype) - zero) * scale
        key = jax.random.key(seed)
        k1, k2, k3, k4, k5 = jax.random.split(key, 5)
        B, S, IC, OC = (4, 512, 512, 512)
        inp = {'input': jax.random.normal(k1, (B, S, IC), dtype=jnp.float32), 'qweight': jax.random.randint(k2, (OC, IC // 2), 0, 32, dtype=jnp.int32), 'scale': jax.random.uniform(k3, (OC, 1), dtype=jnp.float32, minval=0.01, maxval=0.05), 'zero': jax.random.uniform(k4, (OC, 1), dtype=jnp.float32, minval=0.0, maxval=15.0), 'bias': jax.random.normal(k5, (OC,), dtype=jnp.float32)}
        return inp
    _L0_ffn_in = _L0_ffn_setup()
    _d = {'L0_attn_a_x': _L0_attn_a_in['x'], 'L0_attn_a_Wqkv': _L0_attn_a_in['Wqkv'], 'L0_attn_a_bqkv': _L0_attn_a_in['bqkv'], 'L0_attn_a_Wo': _L0_attn_a_in['Wo'], 'L0_attn_a_bo': _L0_attn_a_in['bo'], 'L0_attn_b_wq': _L0_attn_b_in['wq'], 'L0_attn_b_wk': _L0_attn_b_in['wk'], 'L0_attn_b_wv': _L0_attn_b_in['wv'], 'L0_attn_b_wo': _L0_attn_b_in['wo'], 'L0_ffn_qweight': _L0_ffn_in['qweight'], 'L0_ffn_scale': _L0_ffn_in['scale'], 'L0_ffn_zero': _L0_ffn_in['zero'], 'L0_ffn_bias': _L0_ffn_in['bias']}
    _x0 = _d['L0_attn_a_x']
    _d['L0_attn_a_x'] = jax.random.normal(jax.random.fold_in(jax.random.key(seed), 1), (4, 256, 512), dtype=_x0.dtype)
    del _x0
    return _d

def reference(L0_attn_a_x, L0_attn_a_Wqkv, L0_attn_a_bqkv, L0_attn_a_Wo, L0_attn_a_bo, L0_attn_b_wq, L0_attn_b_wk, L0_attn_b_wv, L0_attn_b_wo, L0_ffn_qweight, L0_ffn_scale, L0_ffn_zero, L0_ffn_bias):

    def _L0_attn_a_ref(x, Wqkv, bqkv, Wo, bo):
        import jax, jax.numpy as jnp
        import numpy as np
        H = 512
        D = H // 4
        B, S, C = x.shape
        d = C // 4
        qkv = jnp.einsum('bsc,cf->bsf', x, Wqkv) + bqkv
        qkv = qkv.reshape(B, S, 3, d)
        q, k, v = (qkv[:, :, 0], qkv[:, :, 1], qkv[:, :, 2])
        scale = 1.0 / jnp.sqrt(jnp.float32(d)).astype(x.dtype)
        attn = jnp.einsum('bqd,bkd->bqk', q, k) * scale
        attn = jax.nn.softmax(attn, axis=-1)
        out = jnp.einsum('bqk,bkd->bqd', attn, v)
        return jnp.einsum('bqd,dc->bqc', out, Wo) + bo

    def _L0_attn_b_ref(x, wq, wk, wv, wo):
        import jax, jax.numpy as jnp
        import numpy as np
        B, S, D = (2, 256, 512)
        H = 32
        HD = D // H
        THETA = 10000.0

        def _rope_cos_sin(seq_len, head_dim, theta=THETA):
            inv = 1.0 / theta ** (np.arange(0, head_dim, 2)[:head_dim // 2].astype(np.float32) / head_dim)
            t = np.arange(seq_len)
            f = np.outer(t, inv).astype(np.float32)
            return (jnp.asarray(np.cos(f)), jnp.asarray(np.sin(f)))

        def _apply_rotary(x, cos, sin):
            xr = x.astype(jnp.float32).reshape(*x.shape[:-1], HD // 2, 2)
            x0, x1 = (xr[..., 0], xr[..., 1])
            c = cos[None, :, None, :]
            s = sin[None, :, None, :]
            o0 = x0 * c - x1 * s
            o1 = x0 * s + x1 * c
            return jnp.stack((o0, o1), axis=-1).reshape(*x.shape[:-1], HD)
        b, s, d = x.shape
        q = (x @ wq).reshape(b, s, H, HD)
        k = (x @ wk).reshape(b, s, H, HD)
        v = (x @ wv).reshape(b, s, H, HD)
        cos, sin = _rope_cos_sin(s, HD)
        q = _apply_rotary(q, cos, sin)
        k = _apply_rotary(k, cos, sin)
        scale = 1.0 / jnp.sqrt(jnp.float32(HD))
        scores = jnp.einsum('bqhd,bkhd->bhqk', q, k) * scale
        causal = jnp.tril(jnp.ones((s, s), dtype=bool))
        scores = jnp.where(causal[None, None], scores, jnp.finfo(scores.dtype).min)
        probs = jax.nn.softmax(scores, axis=-1)
        out = jnp.einsum('bhqk,bkhd->bqhd', probs, v).reshape(b, s, d)
        return out @ wo

    def _L0_ffn_ref(input, qweight, scale, zero, bias):
        import jax, jax.numpy as jnp
        import numpy as np
        NIBBLE_MASK = 15

        def _dequant_weight(qweight, scale, zero):
            q = qweight.astype(jnp.int32)
            low = q & NIBBLE_MASK
            high = q >> 4 & NIBBLE_MASK
            OC = q.shape[0]
            w_int = jnp.stack([high, low], axis=-1).reshape(OC, -1)
            return (w_int.astype(scale.dtype) - zero) * scale
        weight = _dequant_weight(qweight, scale, zero).astype(input.dtype)
        out = jnp.einsum('bsi,oi->bso', input, weight) + bias
        return out
    x = L0_attn_a_x
    x = x + _L0_attn_a_ref(_layernorm(x, axis=-1), L0_attn_a_Wqkv, L0_attn_a_bqkv, L0_attn_a_Wo, L0_attn_a_bo)
    x = x + _L0_ffn_ref(_layernorm(x, axis=-1), L0_ffn_qweight, L0_ffn_scale, L0_ffn_zero, L0_ffn_bias)
    x = x + _L0_attn_b_ref(_layernorm(x, axis=-1), L0_attn_b_wq, L0_attn_b_wk, L0_attn_b_wv, L0_attn_b_wo)
    x = x + _L0_ffn_ref(_layernorm(x, axis=-1), L0_ffn_qweight, L0_ffn_scale, L0_ffn_zero, L0_ffn_bias)
    return x

_drawn_inputs = setup_inputs


def setup_inputs(seed=0):
    import zlib

    import numpy as np

    out = dict(_drawn_inputs(seed))
    spreads = {}
    factors = {'L0_attn_a_bqkv': 7.945,
     'L0_attn_a_bo': 6.715,
     'L0_attn_b_wq': 8.0,
     'L0_attn_b_wk': 8.0,
     'L0_attn_b_wv': 3.114,
     'L0_attn_b_wo': 3.146,
     'L0_ffn_zero': 8.0}
    for name, (base, spread) in spreads.items():
        noise = np.random.default_rng([zlib.crc32(name.encode()), seed]).standard_normal(out[name].shape)
        drawn = base * np.exp(spread * noise) if base else spread * noise
        out[name] = jnp.asarray(drawn.astype(out[name].dtype))
    for name, factor in factors.items():
        out[name] = (out[name] * factor).astype(out[name].dtype)
    return out
```

```python
from contextlib import ExitStack

import numpy as np

import concourse.bass as bass
from concourse import mybir

F32 = mybir.dt.float32
F32R = mybir.dt.float32r
BF16 = mybir.dt.bfloat16
I32 = mybir.dt.int32
ALU = mybir.AluOpType
ACT = mybir.ActivationFunctionType
AX = mybir.AxisListType.X

P = 128
B, S, C = 4, 256, 512
NT = S // P
KT = C // P
DA = C // 4
H, HD = 32, 16
THETA = 10000.0
EPS = 1e-5
UH = P // HD
NU = B * KT
GH = 4
NG = UH // GH
Q_PARTS = (0, 0, 0, 1, 1, 2)
K_PARTS = (0, 1, 2, 0, 1, 0)
KROWS = HD * len(Q_PARTS)
SROWS = KROWS + 2
QK_SLOTS = 5
V_SLOTS = 3
MASKED = -1.0e30
RSQRT_MAGIC = float(0x5F3759DF)
BANKS = 8
BANK = 512


def rope_tables():
    inv = 1.0 / THETA ** (np.arange(0, HD, 2)[:HD // 2].astype(np.float32) / HD)
    f = np.outer(np.arange(S), inv).astype(np.float32)
    pair = (np.arange(P) % HD) // 2
    sign = np.where(np.arange(P) % 2 == 0, -1.0, 1.0).astype(np.float32)
    cos = np.cos(f).T[pair]
    sin = np.sin(f).T[pair] * sign[:, None]
    return np.ascontiguousarray(np.stack([cos, sin], 1).astype(np.float32))


def schedule():
    early = [[("LN", 1, b), ("T", 1, b), ("QKV", b), ("SA", b), ("SM", b), ("ET", b), ("OA", b), ("WA", b),
              ("LN", 2, b), ("T", 2, b), ("F", 2, b)] for b in range(B)]
    steps = [("WQ",), ("LN", 1, 0), ("LN", 1, 1), ("T", 1, 0)]
    seen = set(steps)
    extra = [("DQ",), ("WT", 0), ("WT", 1), ("WT", 2), ("WT", 3), ("WB", 0), ("WB", 1), ("WB", 2)]
    last_f = []
    for tau in range(len(early[0]) + 2 * (B - 1)):
        for b in range(B):
            k = tau - 2 * b
            if 0 <= k < len(early[b]):
                s = early[b][k]
                if s[0] in ("F", "T", "LN") and s[1] == 2 and b == 3:
                    last_f.append(s)
                elif s not in seen:
                    steps.append(s)
        if tau >= 1 and extra:
            steps.append(extra.pop(0))
    steps += extra
    steps += [("LN", 3, 0)] + last_f[:1] + [("T", 3, 0)] + [("PROJ", 0), ("VP", 0), ("P1", 0)] + last_f[1:2]
    steps += [("PROJ", 1), ("P2", 0), ("P1", 1), ("P3", 0)] + last_f[2:] + [("P2", 1), ("P3", 1)]
    steps += [("PROJ", 2), ("VP", 1), ("P1", 2)]
    steps += [("PROJ", 3), ("P2", 2), ("P1", 3), ("P3", 2), ("P2", 3), ("P3", 3), ("LN", 3, 1)]
    for g in range(NG):
        steps += [("S", 0, g)]
    steps += [("MT", 0)]
    for g in range(NG):
        steps += [("S", 1, g)]
    steps += [("MT", 1)]
    for i in range(NU):
        b, k = divmod(i, KT)
        fill = [[], [], [], []]
        if i + 4 < NU:
            fill[0] += [("T", 3, b + 1)] if k == 0 else []
            fill[0] += [("PROJ", i + 4)]
            fill[1] += [("VP", (i + 4) // 2)] if k % 2 == 0 else []
            fill[1] += [("P1", i + 4)]
            fill[2] += [("P2", i + 4)]
            fill[3] += [("P3", i + 4)]
        fill[1] += [("NRM", i - 1)] if i else []
        if b:
            if k == 0:
                fill[2] += [("DT", b - 1)]
                fill[3] += [("WO", b - 1)]
            if k == 1:
                fill[0] += [("LN", 4, b - 1)]
            if k == 2:
                fill[0] += [("T", 4, b - 1)]
                fill[2] += [("F", 4, b - 1)]
        if k == 3 and b + 2 < B:
            fill[3] += [("LN", 3, b + 2)]
        for g in range(NG):
            steps.append(("ST", i, g))
            steps += fill[2 * g]
            if i or g:
                steps.append(("PV", *divmod(i * NG + g - 1, NG)))
            if i + 2 < NU:
                steps.append(("S", i + 2, g))
            if g == 0:
                steps += fill[1]
            elif i + 2 < NU:
                steps.append(("MT", i + 2))
            if g == 1:
                steps += fill[3]
    steps += [("PV", NU - 1, NG - 1), ("NRM", NU - 1), ("DT", B - 1), ("WO", B - 1),
              ("LN", 4, B - 1), ("T", 4, B - 1), ("F", 4, B - 1)]
    return steps


JOBS = {"WT": 1, "T": 2, "QKV": 2, "SA": 1, "ET": 1, "OA": 1, "WA": NT, "F": NT, "PROJ": 1, "VP": 1, "MT": 1,
        "PV": 1, "NRM": 1, "DT": 2, "WO": NT}


def hybrid_block_kernel(nc, x, Wqkv, bqkv, Wo, bo, wq, wk, wv, wo, qweight, scale, zero, bias, rope, out):
    steps = schedule()
    count, nth = {}, {}
    for st in steps:
        nth[st] = count.get(st[0], 0)
        count[st[0]] = nth[st] + 1
    bank_of, before, owner, turn, scores_on = {}, {}, [None] * BANKS, 0, False
    taken_by_scores = []
    for st in steps:
        if st[0] == "S" and not scores_on:
            scores_on, taken_by_scores = True, [o for o in owner[:6] if o]
        jobs = [(*st, j) for j in range(JOBS.get(st[0], 0))]
        jobs += [("VA", st[1], 0)] if st[0] == "SA" else []
        for job in jobs:
            turn += 1
            bank = 6 + turn % 2 if scores_on else turn % BANKS
            bank_of[job], before[job], owner[bank] = bank, owner[bank], job

    def job_count(job):
        if job[0] == "VA":
            return nth[("SA", job[1])] + 1
        return nth[job[:-1]] * JOBS[job[0]] + job[-1] + 1

    xt_slot, xt_before, xn_before, holder, xn_holder = {}, {}, {}, {}, {}
    for st in steps:
        if st[0] == "T":
            s, b = st[1:]
            slot = b % 2 if s < 3 else (s - 3)
            xt_slot[st], xt_before[st] = slot, holder.get(slot)
            holder[slot] = {1: ("QKV", b, 1), 2: ("F", 2, b, 1), 3: ("VP", 2 * b + 1, 0), 4: ("F", 4, b, 1)}[s]
        if st[0] == "LN":
            s, b = st[1:]
            slot = b % 2 if s < 3 else 0
            xn_before[st] = xn_holder.get(slot)
            xn_holder[slot] = ("T", s, b, 1)

    def last_reader(job):
        return ("PROJ", job[1] * 2 + 1, 0) if job and job[0] == "VP" else job

    with ExitStack() as ctx:
        def sb(name, shape, dt, where=ctx):
            return where.enter_context(nc.sbuf_tensor(name, shape, dt))

        def sem(name):
            return ctx.enter_context(nc.semaphore(name))

        psum = ctx.enter_context(nc.psum_tensor("psum", [P, BANKS * BANK], F32))

        def bank(k, n=1):
            return psum[:, k * BANK:(k + n) * BANK]

        X = sb("X", [P, B, NT, C], F32)
        wf_hi = sb("wf_hi", [P, KT, C], F32R)
        wf_lo = sb("wf_lo", [P, KT, C], F32R)
        wb_hi = sb("wb_hi", [P, 3, KT, C], F32R)
        wb_lo = sb("wb_lo", [P, 3, KT, C], F32R)
        wo_sb = sb("wo_sb", [P, KT, C], F32)
        XN = sb("XN", [P, 2, NT, C], F32)
        XT_hi = sb("XT_hi", [P, 2, KT, S], F32R)
        XT_lo = sb("XT_lo", [P, 2, KT, S], F32R)
        bias_f = sb("bias_f", [P, C], F32)
        ident = sb("ident", [P, P], F32)
        ident_h = sb("ident_h", [P, P], BF16)
        tri = sb("tri", [P, P], BF16)
        stats = sb("stats", [P, NT, 6], F32)
        mv = sb("mv", [P, NT, 2], F32)
        var = sb("var", [P, NT], F32)
        rstd = sb("rstd", [P, NT], F32)
        newton = sb("newton", [P, NT], F32)

        early = ExitStack()
        wqkv_hi = sb("wqkv_hi", [P, KT, 3 * DA], F32R, early)
        wqkv_lo = sb("wqkv_lo", [P, KT, 3 * DA], F32R, early)
        wo1 = sb("wo1", [P, C], F32, early)
        bias_o = sb("bias_o", [P, C], F32, early)
        bqkv_c = sb("bqkv_c", [P, 3], F32, early)
        stage = sb("stage", [P, 2, KT * C], F32, early)
        q_int = sb("q_int", [P, KT, C // 2], I32, early)
        scale_c = sb("scale_c", [P, KT], F32, early)
        zero_c = sb("zero_c", [P, KT], F32, early)
        qkT = sb("qkT", [P, 2, 2, S], F32, early)
        vT = sb("vT", [P, 2, S], F32, early)
        va = sb("va", [P, 2, NT, DA], F32, early)
        EA = sb("EA", [P, 2, NT, S], F32, early)
        ETs = sb("ETs", [P, 2, NT, S], F32, early)
        OTa = sb("OTa", [P, 2, S], F32, early)
        nmax_a = sb("nmax_a", [P, 2, NT], F32, early)
        sum_a = sb("sum_a", [P, 2, NT], F32, early)
        inv_a = sb("inv_a", [P, 2, NT], F32, early)
        early.close()

        QS = sb("QS", [P, QK_SLOTS, UH, S], BF16)
        KS = sb("KS", [P, QK_SLOTS, UH, S], BF16)
        E = sb("E", [P, 2, GH * 3 * P], F32)
        V = sb("V", [P, V_SLOTS, NT, 2 * UH, 2 * HD], F32)
        parts = sb("parts", [P, 2, 3, 2 * S], BF16)
        SH = sb("SH", [P, 2, 2 * S], F32)
        CC = sb("CC", [P, 2, 2 * S], F32)
        OU = sb("OU", [P, 2, NG, S], F32)
        OT = sb("OT", [P, KT, S], F32)
        table = sb("table", [P, 2, S], F32)
        nmax = sb("nmax", [P, 2, NT, UH], F32)
        mrow = sb("mrow", [UH, 2, 2, S], BF16)
        inv_o = sb("inv_o", [P, NG * NT * GH], F32)

        scratch = nc.dram_tensor("qk_parts", (2, 3, 2, P, S), BF16, kind="Internal").ap()

        made = {k: sem(f"made_{k}") for k in [*JOBS, "VA", "S", "ST"]}
        x_loaded = [sem(f"x_loaded{b}") for b in range(B)]
        wqkv_loaded, small_loaded, q_loaded = sem("wqkv_loaded"), sem("small_loaded"), sem("q_loaded")
        wo1_loaded, wo_loaded, table_loaded = sem("wo1_loaded"), sem("wo_loaded"), sem("table_loaded")
        staged = [sem(f"staged{m}") for m in range(3)]
        consts_ready, consts_cleared = sem("consts_ready"), sem("consts_cleared")
        ones_ready = sem("ones_ready")
        wqkv_hi_ready, wqkv_lo_ready = sem("wqkv_hi_ready"), sem("wqkv_lo_ready")
        wf_hi_ready, wf_lo_ready, dequantised = sem("wf_hi_ready"), sem("wf_lo_ready"), sem("dequantised")
        wb_hi_ready, wb_lo_ready = sem("wb_hi_ready"), sem("wb_lo_ready")
        xn_ready, bias_added = sem("xn_ready"), sem("bias_added")
        xh_ready, xl_ready = sem("xh_ready"), sem("xl_ready")
        qkv_ready, va_ready, nmax_a_ready = sem("qkv_ready"), sem("va_ready"), sem("nmax_a_ready")
        ea_ready, ea_normed, et_ready, oa_ready = sem("ea_ready"), sem("ea_normed"), sem("et_ready"), sem("oa_ready")
        resid_a, resid_f, resid_o = sem("resid_a"), sem("resid_f"), sem("resid_o")
        rope_parts, roped = sem("rope_parts"), sem("roped")
        part1_ready, rest1_ready, part2_ready, part3_ready = sem("part1"), sem("rest1"), sem("part2"), sem("part3")
        v_ready, max_ready, m1_ready, m2_ready = sem("v_ready"), sem("max_ready"), sem("m1_ready"), sem("m2_ready")
        exp_ready, masked, ou_ready, o_ready, ot_ready = (sem("exp_ready"), sem("masked"), sem("ou_ready"),
                                                         sem("o_ready"), sem("ot_ready"))
        parts_stored = [sem(f"parts_stored{i}") for i in range(2)]
        qk_loaded = [sem(f"qk_loaded{i}") for i in range(QK_SLOTS)]
        m_loaded = [sem(f"m_loaded{i}") for i in range(2)]
        out_done = sem("out_done")
        dve_link, pool_link = sem("dve_link"), sem("pool_link")

        released = {"WT": wf_lo_ready, "T": xl_ready, "QKV": qkv_ready, "VA": va_ready, "SA": ea_ready,
                    "ET": et_ready, "OA": oa_ready, "WA": resid_a, "F": resid_f, "PROJ": rope_parts,
                    "VP": v_ready, "MT": m2_ready, "PV": ou_ready, "NRM": o_ready, "DT": ot_ready,
                    "WO": resid_o}

        def wait_job(eng, job):
            eng.wait_ge(made[job[0]], job_count(job))

        def early_over(eng):
            eng.wait_ge(resid_a, B * NT)
            eng.wait_ge(wb_lo_ready, 3)
            eng.wait_ge(wf_lo_ready, KT)

        bqkv_v = bqkv.rearrange("(j p) -> p j", p=P)
        x_v = x.rearrange("b (t p) n -> b p t n", p=P)
        out_v = out.rearrange("b (t p) n -> b p t n", p=P)

        def rows(w):
            return w.rearrange("(k p) n -> p k n", p=P)

        def staging(m):
            return stage[:, m % 2, :].rearrange("p (k n) -> p k n", k=KT)

        block = ctx.enter_context(nc.Block())

        @block.sync
        def _(sp):
            sp.dma_start(X[:, 0], x_v[0]).then_inc(x_loaded[0], 16)
            sp.dma_start(stage[:, 0, 0:KT * 3 * DA].rearrange("p (k n) -> p k n", k=KT),
                         rows(Wqkv)).then_inc(wqkv_loaded, 16)
            sp.dma_start(X[:, 1], x_v[1]).then_inc(x_loaded[1], 16)
            sp.dma_start(bqkv_c[:], bqkv_v, allow_slow_non_contiguous=True).then_inc(small_loaded, 16)
            sp.dma_start(scale_c[:], scale.rearrange("(j p) a -> p (j a)", p=P),
                         allow_slow_non_contiguous=True).then_inc(small_loaded, 16)
            sp.dma_start(zero_c[:], zero.rearrange("(j p) a -> p (j a)", p=P),
                         allow_slow_non_contiguous=True).then_inc(small_loaded, 16)
            sp.dma_start(bias_o[:], bo.partition_broadcast(P)).then_inc(small_loaded, 16)
            sp.dma_start(bias_f[:], bias.partition_broadcast(P)).then_inc(small_loaded, 16)
            sp.dma_start(q_int[:], rows(qweight)).then_inc(q_loaded, 16)
            sp.dma_start(wo1[:], Wo).then_inc(wo1_loaded, 16)
            sp.dma_start(X[:, 2], x_v[2]).then_inc(x_loaded[2], 16)
            sp.dma_start(X[:, 3], x_v[3]).then_inc(x_loaded[3], 16)
            sp.dma_start(wo_sb[:], rows(wo)).then_inc(wo_loaded, 16)
            for m, w in enumerate((wq, wk, wv)):
                if m == 0:
                    sp.wait_ge(dequantised, 1)
                elif m == 1:
                    sp.wait_ge(made["WT"], KT)
                else:
                    sp.wait_ge(wb_lo_ready, 1)
                sp.dma_start(staging(m), rows(w)).then_inc(staged[m], 16)
            early_over(sp)
            sp.dma_start(table[:], rope).then_inc(table_loaded, 16)
            for st in steps:
                if st[0] == "P3":
                    u = st[1]
                    sp.wait_ge(part3_ready, u + 1)
                    if u >= 2:
                        sp.wait_ge(qk_loaded[(u - 2) % QK_SLOTS], 16 * 2 * len(Q_PARTS) * ((u - 2) // QK_SLOTS + 1))
                    sp.dma_start(scratch[u % 2].rearrange("c a d t -> d (c a) t"),
                                 parts[:, u % 2].rearrange("p c (a t) -> p (c a) t", a=2)
                                 ).then_inc(parts_stored[u % 2], 16)
                    sp.wait_ge(parts_stored[u % 2], 16 * (u // 2 + 1))
                    if u >= QK_SLOTS:
                        sp.wait_ge(made["ST"], nth[("ST", u - QK_SLOTS, NG - 1)] + 1)
                    for a, (stack, which) in enumerate(((QS, Q_PARTS), (KS, K_PARTS))):
                        for row, c in enumerate(which):
                            sp.dma_start(stack[row * HD:(row + 1) * HD, u % QK_SLOTS],
                                         scratch[u % 2, c, a].rearrange("(h d) t -> d h t", d=HD)
                                         ).then_inc(qk_loaded[u % QK_SLOTS], 16)
                if st[0] == "MT":
                    u = st[1]
                    sp.wait_ge(m2_ready, nth[st] + 1)
                    sp.wait_ge(m1_ready, nth[st] + 1)
                    for r in range(2):
                        sp.dma_start(QS[KROWS + r:KROWS + r + 1, u % QK_SLOTS], mrow[:, u % 2, r]
                                     ).then_inc(m_loaded[u % 2], 16)
                if st[0] == "F" and st[1] == 4:
                    sp.wait_ge(resid_f, (nth[st] + 1) * NT)
                    sp.dma_start(out_v[st[2]], X[:, st[2]]).then_inc(out_done, 16)
            sp.wait_ge(out_done, 16 * B)

        @block.gpsimd
        def _(pool):
            links = [0]

            def link(ins):
                links[0] += 1
                ins.then_inc(pool_link, 1)
                pool.wait_ge(pool_link, links[0])

            nc.gpsimd.memset(ident[:], 0.0).then_inc(consts_cleared, 1)
            nc.gpsimd.memset(ident_h[:], 0.0).then_inc(consts_cleared, 1)
            nc.gpsimd.memset(tri[:], 0.0).then_inc(consts_cleared, 1)
            pool.wait_ge(consts_cleared, 3)
            for m in (ident, ident_h):
                nc.gpsimd.affine_select(out=m[:], in_=m[:], compare_op=ALU.not_equal, fill=1.0, base=0,
                                        pattern=[[-1, P]], channel_multiplier=1).then_inc(consts_ready, 1)
            nc.gpsimd.affine_select(out=tri[:], in_=tri[:], compare_op=ALU.is_ge, fill=MASKED, base=0,
                                    pattern=[[-1, P]], channel_multiplier=1).then_inc(consts_ready, 1)
            late, biases = False, 0
            for st in steps:
                if st[0] == "LN" and st[1] != 3:
                    biases += NT
                    s, b = st[1:]
                    pool.wait_ge(xn_ready, nth[st] + 1)
                    if s == 1 and b == 0:
                        pool.wait_ge(small_loaded, 16 * 5)
                    for t in range(NT):
                        nc.gpsimd.tensor_tensor(X[:, b, t], X[:, b, t], (bias_o if s == 1 else bias_f)[:], ALU.add
                                                ).then_inc(bias_added, 1)
                if st[0] == "WB":
                    m = st[1]
                    pool.wait_ge(staged[m], 16)
                    pool.wait_ge(wb_hi_ready, m + 1)
                    nc.gpsimd.tensor_tensor(wb_lo[:, m], staging(m), wb_hi[:, m].bitcast(F32), ALU.subtract
                                            ).then_inc(wb_lo_ready, 1)
                if st[0] == "PROJ":
                    u = st[1]
                    if not late:
                        late = True
                        early_over(pool)
                        pool.wait_ge(bias_added, biases)
                        nc.gpsimd.memset(KS[KROWS:P], 1.0).then_inc(ones_ready, 1)
                        pool.wait_ge(ones_ready, 1)
                        nc.gpsimd.memset(V[:], 1.0).then_inc(ones_ready, 1)
                        pool.wait_ge(table_loaded, 16)
                    pool.wait_ge(rope_parts, u + 1)
                    sh = SH[:, u % 2].rearrange("p (a t) -> p a t", a=2)
                    link(nc.gpsimd.tensor_tensor(sh, sh, table[:, 1:2, :].to_broadcast((P, 2, S)), ALU.mult))
                    nc.gpsimd.tensor_tensor(SH[:, u % 2], SH[:, u % 2], CC[:, u % 2], ALU.add).then_inc(roped, 1)
                if st[0] == "P1":
                    u = st[1]
                    pool.wait_ge(roped, u + 1)
                    pool.wait_ge(part1_ready, u + 1)
                    nc.gpsimd.tensor_tensor(SH[:, u % 2], SH[:, u % 2], parts[:, u % 2, 0], ALU.subtract
                                            ).then_inc(rest1_ready, 1)
                if st[0] == "ST":
                    n = nth[st]
                    pool.wait_ge(exp_ready, n + 1)
                    for at, width in ((0, S), (GH * S, P)):
                        e = E[:, n % 2, at:at + GH * width].rearrange("p (h q) -> p h q", h=GH)[:, :, 0:P]
                        last = nc.gpsimd.affine_select(out=e, in_=e, compare_op=ALU.is_ge, fill=0.0, base=0,
                                                       pattern=[[0, GH], [1, P]], channel_multiplier=-1)
                    last.then_inc(masked, 1)

        @block.scalar
        def _(act):
            late = False

            def copy(out_, in_):
                return nc.scalar.activation(out_, in_, ACT.Copy)

            for st in steps:
                k = st[0]
                if k == "WQ":
                    act.wait_ge(wqkv_loaded, 16)
                    copy(wqkv_hi[:].rearrange("p k n -> p (k n)"), stage[:, 0, 0:KT * 3 * DA]
                         ).then_inc(wqkv_hi_ready, 1)
                elif k == "WB":
                    m = st[1]
                    act.wait_ge(staged[m], 16)
                    copy(wb_hi[:, m], staging(m)).then_inc(wb_hi_ready, 1)
                elif k == "WT":
                    wait_job(act, (*st, 0))
                    copy(wf_hi[:, st[1]], bank(bank_of[(*st, 0)])).then_inc(wf_hi_ready, 1)
                elif k == "T":
                    slot = xt_slot[st]
                    for j in range(2):
                        wait_job(act, (*st, j))
                        if j == 0 and xt_before[st]:
                            wait_job(act, last_reader(xt_before[st]))
                        copy(XT_hi[:, slot, 2 * j:2 * j + 2].rearrange("p k n -> p (k n)"),
                             bank(bank_of[(*st, j)])).then_inc(xh_ready, 1)
                elif k == "QKV":
                    b = st[1]
                    wait_job(act, (*st, 0))
                    if b == 0:
                        act.wait_ge(small_loaded, 16 * 5)
                    if b >= 2:
                        wait_job(act, ("SA", b - 2, 0))
                    ps = bank(bank_of[(*st, 0)])
                    nc.scalar.activation(qkT[:, b % 2, 0], ps[:, 0:S], ACT.Identity, bias=bqkv_c[:, 0:1])
                    nc.scalar.activation(qkT[:, b % 2, 1], ps[:, S:2 * S], ACT.Identity, bias=bqkv_c[:, 1:2]
                                         ).then_inc(qkv_ready, 1)
                    wait_job(act, (*st, 1))
                    if b >= 2:
                        wait_job(act, ("VA", b - 2, 0))
                    nc.scalar.activation(vT[:, b % 2], bank(bank_of[(*st, 1)])[:, 0:S], ACT.Identity,
                                         bias=bqkv_c[:, 2:3]).then_inc(qkv_ready, 1)
                elif k == "SA":
                    b = st[1]
                    wait_job(act, ("VA", b, 0))
                    if b >= 2:
                        wait_job(act, ("OA", b - 2, 0))
                    copy(va[:, b % 2].rearrange("p t d -> p (t d)"), bank(bank_of[("VA", b, 0)])[:, 0:NT * DA]
                         ).then_inc(va_ready, 1)
                elif k == "SM":
                    b = st[1]
                    act.wait_ge(nmax_a_ready, b + 1)
                    if b >= 2:
                        wait_job(act, ("ET", b - 2, 0))
                    ps = bank(bank_of[("SA", b, 0)])
                    for t in range(NT):
                        last = nc.scalar.activation(EA[:, b % 2, t], ps[:, t * S:(t + 1) * S], ACT.Exp,
                                                    bias=nmax_a[:, b % 2, t:t + 1], scale=float(DA) ** -0.5,
                                                    accum_out=sum_a[:, b % 2, t:t + 1])
                    last.then_inc(ea_ready, 1)
                elif k == "ET":
                    b = st[1]
                    wait_job(act, (*st, 0))
                    if b >= 2:
                        wait_job(act, ("OA", b - 2, 0))
                    copy(ETs[:, b % 2].rearrange("p k q -> p (k q)"), bank(bank_of[(*st, 0)])).then_inc(et_ready, 1)
                elif k == "OA":
                    b = st[1]
                    wait_job(act, (*st, 0))
                    if b >= 2:
                        wait_job(act, ("WA", b - 2, NT - 1))
                    copy(OTa[:, b % 2], bank(bank_of[(*st, 0)])[:, 0:S]).then_inc(oa_ready, 1)
                elif k == "P1":
                    u = st[1]
                    if not late:
                        late = True
                        early_over(act)
                    act.wait_ge(roped, u + 1)
                    if u >= 2:
                        act.wait_ge(parts_stored[u % 2], 16 * (u // 2))
                    copy(parts[:, u % 2, 0], SH[:, u % 2]).then_inc(part1_ready, 1)
                elif k == "P2":
                    u = st[1]
                    act.wait_ge(rest1_ready, u + 1)
                    copy(parts[:, u % 2, 1], SH[:, u % 2]).then_inc(part2_ready, 1)
                elif k == "VP":
                    v = st[1]
                    wait_job(act, (*st, 0))
                    if v == 0:
                        act.wait_ge(ones_ready, 2)
                    if v >= V_SLOTS:
                        wait_job(act, ("PV", 2 * (v - V_SLOTS) + 1, NG - 1, 0))
                    copy(V[:, v % V_SLOTS, :, :, 0:HD],
                         bank(bank_of[(*st, 0)]).rearrange("p (t h d) -> p t h d", t=NT, d=HD)).then_inc(v_ready, 1)
                elif k == "MT":
                    u = st[1]
                    wait_job(act, (*st, 0))
                    if u >= 2:
                        act.wait_ge(m_loaded[u % 2], 32 * (u // 2))
                    copy(mrow[:, u % 2, 0], bank(bank_of[(*st, 0)])[0:UH, 0:S]).then_inc(m1_ready, 1)
                elif k == "ST":
                    n = nth[st]
                    act.wait_ge(made["ST"], n + 1)
                    if n >= 2:
                        wait_job(act, ("PV", *divmod(n - 2, NG), 0))
                    nc.scalar.activation(E[:, n % 2], bank(3, 3), ACT.Exp, scale=float(HD) ** -0.5
                                         ).then_inc(exp_ready, 1)
                elif k == "PV":
                    u, g = st[1:]
                    wait_job(act, (*st, 0))
                    if u >= 2:
                        wait_job(act, ("NRM", u - 2, 0))
                    copy(OU[:, u % 2, g], bank(bank_of[(*st, 0)])[:, 0:S]).then_inc(ou_ready, 1)
                elif k == "DT":
                    b = st[1]
                    for j in range(2):
                        wait_job(act, (*st, j))
                        if b and j == 0:
                            wait_job(act, ("WO", b - 1, NT - 1))
                        copy(OT[:, 2 * j:2 * j + 2].rearrange("p k n -> p (k n)"), bank(bank_of[(*st, j)])
                             ).then_inc(ot_ready, 1)

        @block.vector
        def _(dve):
            links = [0]
            late = False
            bias_n = {}
            for st in steps:
                if st[0] == "LN" and st[1] != 3:
                    bias_n[st[1:]] = (len(bias_n) + 1) * NT

            def link(ins):
                links[0] += 1
                ins.then_inc(dve_link, 1)
                dve.wait_ge(dve_link, links[0])

            def add_residual(job, b, t, sem_):
                wait_job(dve, job)
                nc.vector.tensor_tensor(X[:, b, t], X[:, b, t], bank(bank_of[job]), ALU.add).then_inc(sem_, 1)

            for st in steps:
                k = st[0]
                if k == "WQ":
                    dve.wait_ge(wqkv_loaded, 16)
                    dve.wait_ge(wqkv_hi_ready, 1)
                    nc.vector.tensor_tensor(wqkv_lo[:].rearrange("p k n -> p (k n)"), stage[:, 0, 0:KT * 3 * DA],
                                            wqkv_hi[:].bitcast(F32).rearrange("p k n -> p (k n)"), ALU.subtract
                                            ).then_inc(wqkv_lo_ready, 1)
                elif k == "DQ":
                    dve.wait_ge(q_loaded, 16)
                    dve.wait_ge(small_loaded, 16 * 5)
                    w_int = staging(0).bitcast(I32)
                    dve.wait_ge(wqkv_lo_ready, 1)
                    w = w_int.rearrange("p j (i e) -> p j i e", e=2)
                    nc.vector.tensor_scalar(w[:, :, :, 0], q_int[:], 4, 15, ALU.logical_shift_right, ALU.bitwise_and)
                    link(nc.vector.tensor_scalar(w[:, :, :, 1], q_int[:], 15, None, ALU.bitwise_and))
                    for j in range(KT):
                        last = nc.vector.tensor_scalar(staging(1)[:, j], w_int[:, j],
                                                       zero_c[:, j:j + 1], scale_c[:, j:j + 1],
                                                       ALU.subtract, ALU.mult)
                    last.then_inc(dequantised, 1)
                elif k == "WT":
                    dve.wait_ge(wf_hi_ready, st[1] + 1)
                    nc.vector.tensor_tensor(wf_lo[:, st[1]], bank(bank_of[(*st, 0)]), wf_hi[:, st[1]].bitcast(F32),
                                            ALU.subtract).then_inc(wf_lo_ready, 1)
                elif k == "LN":
                    s, b = st[1:]
                    slot = b % 2 if s < 3 else 0
                    if s == 1:
                        dve.wait_ge(x_loaded[b], 16)
                    elif s == 2:
                        dve.wait_ge(resid_a, (b + 1) * NT)
                    elif s == 3:
                        dve.wait_ge(resid_f, job_count(("F", 2, b, NT - 1)))
                    else:
                        dve.wait_ge(resid_o, (b + 1) * NT)
                    nc.vector.bn_stats(stats[:, 0], X[:, b, 0])
                    link(nc.vector.bn_stats(stats[:, 1], X[:, b, 1]))
                    nc.vector.bn_aggr(mv[:, 0], stats[:, 0])
                    link(nc.vector.bn_aggr(mv[:, 1], stats[:, 1]))
                    link(nc.vector.tensor_scalar(var[:], mv[:, :, 1], EPS, None, ALU.add))
                    link(nc.vector.tensor_scalar(rstd[:].bitcast(I32), var[:].bitcast(I32), -0.5, RSQRT_MAGIC,
                                                 ALU.mult, ALU.add))
                    for _ in range(3):
                        link(nc.vector.scalar_tensor_tensor(newton[:], rstd[:], -0.5, rstd[:], ALU.mult, ALU.mult))
                        link(nc.vector.tensor_tensor(newton[:], newton[:], var[:], ALU.mult))
                        link(nc.vector.scalar_tensor_tensor(rstd[:], newton[:], 1.5, rstd[:], ALU.add, ALU.mult))
                    if xn_before[st]:
                        wait_job(dve, xn_before[st])
                    for t in range(NT):
                        last = nc.vector.tensor_scalar(XN[:, slot, t], X[:, b, t], mv[:, t, 0:1], rstd[:, t:t + 1],
                                                       ALU.subtract, ALU.mult)
                    last.then_inc(xn_ready, 1)
                elif k == "T":
                    slot = xt_slot[st]
                    for j in range(2):
                        dve.wait_ge(xh_ready, nth[st] * 2 + j + 1)
                        if j == 0 and xt_before[st]:
                            wait_job(dve, last_reader(xt_before[st]))
                        nc.vector.tensor_tensor(XT_lo[:, slot, 2 * j:2 * j + 2].rearrange("p k n -> p (k n)"),
                                                bank(bank_of[(*st, j)]),
                                                XT_hi[:, slot, 2 * j:2 * j + 2].bitcast(F32).rearrange("p k n -> p (k n)"),
                                                ALU.subtract).then_inc(xl_ready, 1)
                elif k == "SA":
                    b = st[1]
                    wait_job(dve, (*st, 0))
                    if b >= 2:
                        dve.wait_ge(ea_ready, b - 1)
                    link(nc.vector.tensor_reduce(nmax_a[:, b % 2], bank(bank_of[(*st, 0)]).rearrange(
                        "p (t k) -> p t k", t=NT), AX, ALU.max))
                    nc.vector.tensor_scalar(nmax_a[:, b % 2], nmax_a[:, b % 2], -float(DA) ** -0.5, None, ALU.mult
                                            ).then_inc(nmax_a_ready, 1)
                elif k == "SM":
                    b = st[1]
                    dve.wait_ge(ea_ready, b + 1)
                    link(nc.vector.reciprocal(inv_a[:, b % 2], sum_a[:, b % 2]))
                    for t in range(NT):
                        last = nc.vector.tensor_scalar(EA[:, b % 2, t], EA[:, b % 2, t], inv_a[:, b % 2, t:t + 1], None,
                                                       ALU.mult)
                    last.then_inc(ea_normed, 1)
                elif k == "WA":
                    b = st[1]
                    dve.wait_ge(bias_added, bias_n[(1, b)])
                    for t in range(NT):
                        add_residual((*st, t), b, t, resid_a)
                elif k == "F":
                    b = st[2]
                    dve.wait_ge(bias_added, bias_n[(st[1], b)])
                    for t in range(NT):
                        add_residual((*st, t), b, t, resid_f)
                elif k == "WO":
                    for t in range(NT):
                        add_residual((*st, t), st[1], t, resid_o)
                elif k == "PROJ":
                    u = st[1]
                    if not late:
                        late = True
                        early_over(dve)
                        dve.wait_ge(table_loaded, 16)
                    wait_job(dve, (*st, 0))
                    if u >= 2:
                        dve.wait_ge(part3_ready, u - 1)
                        dve.wait_ge(roped, u - 1)
                    ps = bank(bank_of[(*st, 0)])
                    nc.vector.stream_shuffle(SH[:, u % 2], ps, [i ^ 1 for i in range(32)])
                    nc.vector.tensor_tensor(CC[:, u % 2].rearrange("p (a t) -> p a t", a=2),
                                            ps.rearrange("p (a t) -> p a t", a=2),
                                            table[:, 0:1, :].to_broadcast((P, 2, S)), ALU.mult
                                            ).then_inc(rope_parts, 1)
                elif k == "P3":
                    u = st[1]
                    dve.wait_ge(part2_ready, u + 1)
                    nc.vector.tensor_tensor(parts[:, u % 2, 2], SH[:, u % 2], parts[:, u % 2, 1], ALU.subtract
                                            ).then_inc(part3_ready, 1)
                elif k == "S":
                    u, g = st[1:]
                    dve.wait_ge(made["S"], nth[st] + 1)
                    if g == 0 and u >= 2:
                        wait_job(dve, ("MT", u - 2, 0))
                    nc.vector.tensor_reduce(nmax[:, u % 2, 0, g * GH:(g + 1) * GH],
                                            bank(0).rearrange("p (h k) -> p h k", h=GH), AX, ALU.max, negate=True)
                    nc.vector.tensor_reduce(nmax[:, u % 2, 1, g * GH:(g + 1) * GH],
                                            bank(1, 2).rearrange("p (h k) -> p h k", h=GH), AX, ALU.max, negate=True
                                            ).then_inc(max_ready, 1)
                elif k == "MT":
                    u = st[1]
                    dve.wait_ge(m1_ready, nth[st] + 1)
                    nc.vector.tensor_tensor(mrow[:, u % 2, 1], bank(bank_of[(*st, 0)])[0:UH, 0:S], mrow[:, u % 2, 0],
                                            ALU.subtract).then_inc(m2_ready, 1)
                elif k == "NRM":
                    u = st[1]
                    b, m = divmod(u, KT)
                    wait_job(dve, (*st, 0))
                    ps = bank(bank_of[(*st, 0)]).rearrange("p (g t h d) -> p g t h d", g=NG, t=NT, h=GH)
                    inv = inv_o[:].rearrange("p (g t h) -> p g t h", g=NG, t=NT)
                    link(nc.vector.reciprocal(inv, ps[:, :, :, :, HD]))
                    if m == 0 and b:
                        wait_job(dve, ("DT", b - 1, 1))
                    for t in range(NT):
                        o = XN[:, 1, t, m * P:(m + 1) * P].rearrange("p (g h d) -> p g h d", g=NG, h=GH)
                        last = nc.vector.tensor_tensor(
                            o, ps[:, :, t, :, 0:HD],
                            inv[:, :, t, :].unsqueeze(3).to_broadcast((P, NG, GH, HD)), ALU.mult)
                    last.then_inc(o_ready, 1)

        @block.tensor
        def _(pe):
            def take(job):
                if before[job]:
                    pe.wait_ge(released[before[job][0]], job_count(before[job]))
                return bank(bank_of[job])

            def three_pass(out_, stat, mov, first, last):
                nc.tensor.matmul(out_, stat[0], mov[1], start=first, stop=False)
                nc.tensor.matmul(out_, stat[1], mov[0], start=False, stop=False)
                return nc.tensor.matmul(out_, stat[0], mov[0], start=False, stop=last)

            scores_on = False
            for st in steps:
                k = st[0]
                if k == "WT":
                    if st[1] == 0:
                        pe.wait_ge(dequantised, 1)
                    ps = take((*st, 0))
                    for j in range(KT):
                        last = nc.tensor.transpose(ps[:, j * P:(j + 1) * P],
                                                   staging(1)[:, j, st[1] * P:(st[1] + 1) * P], ident[:])
                    last.then_inc(made[k], 1)
                elif k == "T":
                    s, b = st[1:]
                    slot = b % 2 if s < 3 else 0
                    if nth[st] == 0:
                        pe.wait_ge(consts_ready, 3)
                    pe.wait_ge(xn_ready, nth[("LN", s, b)] + 1)
                    for j in range(2):
                        ps = take((*st, j))
                        for kk in range(2):
                            for t in range(NT):
                                c = (2 * j + kk) * P
                                last = nc.tensor.transpose(ps[:, kk * S + t * P:kk * S + (t + 1) * P],
                                                           XN[:, slot, t, c:c + P], ident[:])
                        last.then_inc(made[k], 1)
                elif k == "QKV":
                    b = st[1]
                    pe.wait_ge(xl_ready, (nth[("T", 1, b)] + 1) * 2)
                    pe.wait_ge(xh_ready, (nth[("T", 1, b)] + 1) * 2)
                    pe.wait_ge(wqkv_lo_ready, 1)
                    for j, blocks in enumerate(((0, 1), (2,))):
                        ps = take((*st, j))
                        for i, m in enumerate(blocks):
                            for kt in range(KT):
                                last = three_pass(ps[:, i * S:(i + 1) * S],
                                                  [w[:, kt, m * DA:(m + 1) * DA] for w in (wqkv_hi, wqkv_lo)],
                                                  [xt[:, b % 2, kt] for xt in (XT_hi, XT_lo)],
                                                  kt == 0, kt == KT - 1)
                        last.then_inc(made[k], 1)
                elif k == "SA":
                    b = st[1]
                    pe.wait_ge(qkv_ready, 2 * (b + 1))
                    ps = take((*st, 0))
                    for t in range(NT):
                        last = nc.tensor.matmul(ps[:, t * S:(t + 1) * S], qkT[:, b % 2, 0, t * P:(t + 1) * P],
                                                qkT[:, b % 2, 1], start=True, stop=True)
                    last.then_inc(made[k], 1)
                    ps = take(("VA", b, 0))
                    for t in range(NT):
                        last = nc.tensor.transpose(ps[:, t * DA:(t + 1) * DA], vT[:, b % 2, t * P:(t + 1) * P], ident[:])
                    last.then_inc(made["VA"], 1)
                elif k == "ET":
                    b = st[1]
                    pe.wait_ge(ea_normed, b + 1)
                    ps = take((*st, 0))
                    for kt in range(NT):
                        for t in range(NT):
                            last = nc.tensor.transpose(ps[:, kt * S + t * P:kt * S + (t + 1) * P],
                                                       EA[:, b % 2, t, kt * P:(kt + 1) * P], ident[:])
                    last.then_inc(made[k], 1)
                elif k == "OA":
                    b = st[1]
                    pe.wait_ge(et_ready, b + 1)
                    pe.wait_ge(va_ready, b + 1)
                    ps = take((*st, 0))
                    for kt in range(NT):
                        last = nc.tensor.matmul(ps[:, 0:S], va[:, b % 2, kt], ETs[:, b % 2, kt],
                                                start=kt == 0, stop=kt == NT - 1)
                    last.then_inc(made[k], 1)
                elif k == "WA":
                    b = st[1]
                    pe.wait_ge(oa_ready, b + 1)
                    if b == 0:
                        pe.wait_ge(wo1_loaded, 16)
                    for t in range(NT):
                        ps = take((*st, t))
                        nc.tensor.matmul(ps, OTa[:, b % 2, t * P:(t + 1) * P], wo1[:], start=True, stop=True
                                         ).then_inc(made[k], 1)
                elif k == "F":
                    s, b = st[1:]
                    tn = nth[("T", s, b)]
                    slot = xt_slot[("T", s, b)]
                    pe.wait_ge(xl_ready, (tn + 1) * 2)
                    pe.wait_ge(xh_ready, (tn + 1) * 2)
                    if nth[st] == 0:
                        pe.wait_ge(wf_hi_ready, KT)
                        pe.wait_ge(wf_lo_ready, KT)
                    for t in range(NT):
                        ps = take((*st, t))
                        for kt in range(KT):
                            last = three_pass(ps, [xt[:, slot, kt, t * P:(t + 1) * P] for xt in (XT_hi, XT_lo)],
                                              [w[:, kt] for w in (wf_hi, wf_lo)], kt == 0, kt == KT - 1)
                        last.then_inc(made[k], 1)
                elif k == "PROJ":
                    u = st[1]
                    b, m = divmod(u, KT)
                    pe.wait_ge(xl_ready, (nth[("T", 3, b)] + 1) * 2)
                    pe.wait_ge(xh_ready, (nth[("T", 3, b)] + 1) * 2)
                    if u == 0:
                        pe.wait_ge(wb_hi_ready, 3)
                        pe.wait_ge(wb_lo_ready, 3)
                    ps = take((*st, 0))
                    for a in range(2):
                        for kt in range(KT):
                            last = three_pass(ps[:, a * S:(a + 1) * S],
                                              [w[:, a, kt, m * P:(m + 1) * P] for w in (wb_hi, wb_lo)],
                                              [xt[:, 0, kt] for xt in (XT_hi, XT_lo)], kt == 0, kt == KT - 1)
                    last.then_inc(made[k], 1)
                elif k == "VP":
                    m = st[1] % 2
                    ps = take((*st, 0))
                    for t in range(NT):
                        for kt in range(KT):
                            last = three_pass(ps[:, t * S:(t + 1) * S],
                                              [xt[:, 0, kt, t * P:(t + 1) * P] for xt in (XT_hi, XT_lo)],
                                              [w[:, 2, kt, m * S:(m + 1) * S] for w in (wb_hi, wb_lo)],
                                              kt == 0, kt == KT - 1)
                    last.then_inc(made[k], 1)
                elif k == "S":
                    u, g = st[1:]
                    slot = u % QK_SLOTS
                    pe.wait_ge(qk_loaded[slot], 16 * 2 * len(Q_PARTS) * (u // QK_SLOTS + 1))
                    if not scores_on:
                        scores_on = True
                        for job in taken_by_scores:
                            pe.wait_ge(released[job[0]], job_count(job))
                    if nth[st]:
                        pe.wait_ge(max_ready, nth[st])
                    nc.tensor.matmul(bank(0).rearrange("p (h k) -> p h k", h=GH), ident_h[:],
                                     tri[:].unsqueeze(1).to_broadcast((P, GH, P)),
                                     start=True, stop=False, skip_group_check=True)
                    for half in range(2):
                        nc.tensor.matmul(bank(1 + half).rearrange("p (h k) -> p h k", h=2)[:, :, P:S], ident_h[:],
                                         tri[:].unsqueeze(1).to_broadcast((P, 2, P)),
                                         start=True, stop=False, skip_group_check=True)
                    for j in range(GH):
                        h = g * GH + j
                        nc.tensor.matmul(bank(0)[:, j * P:(j + 1) * P], QS[0:KROWS, slot, h, 0:P],
                                         KS[0:KROWS, slot, h, 0:P], start=False, stop=True, skip_group_check=True)
                        last = nc.tensor.matmul(bank(1, 2)[:, j * S:(j + 1) * S], QS[0:KROWS, slot, h, P:S],
                                                KS[0:KROWS, slot, h, :], start=False, stop=True, skip_group_check=True)
                    last.then_inc(made[k], 1)
                elif k == "MT":
                    u = st[1]
                    pe.wait_ge(max_ready, nth[("S", u, NG - 1)] + 1)
                    ps = take((*st, 0))
                    for t in range(NT):
                        last = nc.tensor.transpose(ps[0:UH, t * P:(t + 1) * P], nmax[:, u % 2, t], ident[:])
                    last.then_inc(made[k], 1)
                elif k == "ST":
                    u, g = st[1:]
                    slot = u % QK_SLOTS
                    if g == 0:
                        pe.wait_ge(m_loaded[u % 2], 32 * (u // 2 + 1))
                    if u == 0 and g == 0:
                        pe.wait_ge(ones_ready, 2)
                    if nth[st]:
                        pe.wait_ge(exp_ready, nth[st])
                    for j in range(GH):
                        h = g * GH + j
                        nc.tensor.matmul(bank(3, 2)[:, j * S:(j + 1) * S], KS[0:SROWS, slot, h, 0:P],
                                         QS[0:SROWS, slot, h, :], start=True, stop=True)
                        last = nc.tensor.matmul(bank(5)[:, j * P:(j + 1) * P], KS[0:SROWS, slot, h, P:S],
                                                QS[0:SROWS, slot, h, P:S], start=True, stop=True)
                    last.then_inc(made[k], 1)
                elif k == "PV":
                    u, g = st[1:]
                    n = u * NG + g
                    pe.wait_ge(masked, n + 1)
                    pe.wait_ge(v_ready, u // 2 + 1)
                    ps = take((*st, 0))
                    for kt in range(NT):
                        for j in range(GH):
                            v = V[:, (u // 2) % V_SLOTS, kt, (u % 2) * UH + g * GH + j]
                            at = j * S if kt == 0 else GH * S + j * P
                            last = nc.tensor.matmul(ps[j * 32:(j + 1) * 32, kt * P:S], v,
                                                    E[:, n % 2, at:at + S - kt * P],
                                                    start=kt == 0, stop=kt == NT - 1, skip_group_check=True)
                    last.then_inc(made[k], 1)
                elif k == "NRM":
                    u = st[1]
                    pe.wait_ge(ou_ready, (u + 1) * NG)
                    ps = take((*st, 0))
                    for g in range(NG):
                        for t in range(NT):
                            c = (g * NT + t) * P
                            last = nc.tensor.transpose(ps[:, c:c + P], OU[:, u % 2, g, t * P:(t + 1) * P], ident[:])
                    last.then_inc(made[k], 1)
                elif k == "DT":
                    b = st[1]
                    pe.wait_ge(o_ready, (b + 1) * KT)
                    for j in range(2):
                        ps = take((*st, j))
                        for kk in range(2):
                            for t in range(NT):
                                c = (2 * j + kk) * P
                                last = nc.tensor.transpose(ps[:, kk * S + t * P:kk * S + (t + 1) * P],
                                                           XN[:, 1, t, c:c + P], ident[:])
                        last.then_inc(made[k], 1)
                elif k == "WO":
                    b = st[1]
                    pe.wait_ge(ot_ready, (b + 1) * 2)
                    if b == 0:
                        pe.wait_ge(wo_loaded, 16)
                    for t in range(NT):
                        ps = take((*st, t))
                        for kt in range(KT):
                            last = nc.tensor.matmul(ps, OT[:, kt, t * P:(t + 1) * P], wo_sb[:, kt],
                                                    start=kt == 0, stop=kt == KT - 1)
                        last.then_inc(made[k], 1)


_INS = ["L0_attn_a_x", "L0_attn_a_Wqkv", "L0_attn_a_bqkv", "L0_attn_a_Wo", "L0_attn_a_bo", "L0_attn_b_wq",
        "L0_attn_b_wk", "L0_attn_b_wv", "L0_attn_b_wo", "L0_ffn_qweight", "L0_ffn_scale", "L0_ffn_zero",
        "L0_ffn_bias"]


def kernel(**inputs):
    import concourse.bacc as bacc
    from concourse.bass_utils import run_bass_kernel_spmd

    nc = bacc.Bacc("TRN2", target_bir_lowering=False, num_devices=1)
    arrays = {n: np.ascontiguousarray(inputs[n]) for n in _INS}
    arrays["rope_table"] = rope_tables()
    args = [nc.dram_tensor(n, a.shape, mybir.dt.from_np(a.dtype), kind="ExternalInput").ap()
            for n, a in arrays.items()]
    out = nc.dram_tensor("out", (B, S, C), F32, kind="ExternalOutput").ap()
    hybrid_block_kernel(nc, *args, out)
    r = run_bass_kernel_spmd(nc, [arrays], core_ids=[0])
    return r.results[0]["out"]
```

```python
from contextlib import ExitStack

import numpy as np

import concourse.bass as bass
from concourse import mybir

F32 = mybir.dt.float32
F32R = mybir.dt.float32r
BF16 = mybir.dt.bfloat16
I32 = mybir.dt.int32
ALU = mybir.AluOpType
ACT = mybir.ActivationFunctionType
AX = mybir.AxisListType.X

P = 128
B, S, C = 4, 256, 512
NT = S // P
KT = C // P
DA = C // 4
H, HD = 32, 16
THETA = 10000.0
EPS = 1e-5
UH = P // HD
NU = B * KT
GH = 4
NG = UH // GH
Q_PARTS = (0, 0, 0, 1, 1, 2)
K_PARTS = (0, 1, 2, 0, 1, 0)
KROWS = HD * len(Q_PARTS)
SROWS = KROWS + 2
QK_SLOTS = 4
V_SLOTS = 3
MASKED = -1.0e30
RSQRT_MAGIC = float(0x5F3759DF - (1 << 30) - (1 << 22))
BANKS = 8
BANK = 512


def rope_tables():
    inv = 1.0 / THETA ** (np.arange(0, HD, 2)[:HD // 2].astype(np.float32) / HD)
    f = np.outer(np.arange(S), inv).astype(np.float32)
    pair = (np.arange(P) % HD) // 2
    sign = np.where(np.arange(P) % 2 == 0, -1.0, 1.0).astype(np.float32)
    cos = np.cos(f).T[pair]
    sin = np.sin(f).T[pair] * sign[:, None]
    return np.ascontiguousarray(np.stack([cos, sin], 1).astype(np.float32))


def schedule():
    chain = [("LN", 1), ("T", 1), ("QKV",), ("SA",), ("SM",), ("ET",), ("OA",), ("WA",), ("LN", 2), None,
             ("T", 2), ("F", 2, 0), ("F", 2, 1)]
    beside = {0: [("LN", 1, 1), ("WQ",), ("DQ",)], 2: [("WT", 0)], 3: [("WT", 1)], 4: [("WT", 2)], 5: [("WT", 3)],
              6: [("WB", 0)], 7: [("WB", 1)], 8: [("WB", 2)],
              13: [("LN", 3, 0)], 15: [("T", 3, 0), ("PROJ", 0)], 16: [("PROJ", 1), ("P1", 0)],
              17: [("VP", 0), ("P2", 0), ("P1", 1)], 18: [("P3", 0), ("PROJ", 2), ("P2", 1), ("LN", 3, 1)]}
    steps = []
    for turn in range(len(chain) + 2 * (B - 1)):
        for b in range(B):
            k = turn - 2 * b
            if 0 <= k < len(chain) and chain[k]:
                st = chain[k]
                st = (st[0], b) if len(st) == 1 else (*st[:2], b, *st[2:])
                if st not in steps:
                    steps.append(st)
        steps += beside.get(turn, [])
    steps += [("P3", 1), ("P1", 2), ("PROJ", 3), ("S", 0, 0), ("P2", 2), ("VP", 1), ("S", 0, 1), ("P3", 2), ("P1", 3),
              ("T", 3, 1), ("MT", 0), ("S", 1, 0), ("P2", 3), ("S", 1, 1)]
    for i in range(NU):
        b, k = divmod(i, KT)
        nxt = i + 4 < NU
        steps += [("ST", i, 0)]
        if i + 1 < NU:
            steps += [("MT", i + 1)]
        if k == 0 and i and nxt:
            steps += [("T", 3, b + 1)]
        if i + 3 < NU:
            steps += [("P2", i + 3)] if i else []
            steps += [("P3", i + 3)]
        if nxt:
            steps += [("PROJ", i + 4)]
        if i:
            steps += [("PV", i - 1, 1)]
        if i + 2 < NU:
            steps += [("S", i + 2, 0)]
        if b and k == 1:
            steps += [("WO", b - 1, 0)]
        if b and k == 3:
            steps += [("T", 4, b - 1), ("F", 4, b - 1, 0)]
        if nxt and k % 2 == 0:
            steps += [("VP", (i + 4) // 2)]
        if i:
            steps += [("NRM", i - 1)]
        steps += [("ST", i, 1)]
        if b and k == 0:
            steps += [("DT", b - 1)]
        if b and k == 1:
            steps += [("WO", b - 1, 1)]
        if b and k == 2:
            steps += [("LN", 4, b - 1)]
        if b and k == 3:
            steps += [("F", 4, b - 1, 1)]
        if k == 3 and b + 2 < B:
            steps += [("LN", 3, b + 2)]
        steps += [("PV", i, 0)]
        if i + 2 < NU:
            steps += [("S", i + 2, 1)]
        if nxt:
            steps += [("P1", i + 4)]
    last = B - 1
    return steps + [("PV", NU - 1, 1), ("NRM", NU - 1), ("DT", last), ("WO", last, 0), ("WO", last, 1),
                    ("LN", 4, last), ("T", 4, last), ("F", 4, last, 0), ("F", 4, last, 1)]


JOBS = {"WT": 1, "T": 2, "QKV": 2, "SA": 1, "ET": 1, "OA": 1, "WA": NT, "F": 1, "PROJ": 1, "VP": 1, "MT": 1,
        "PV": 1, "NRM": 1, "DT": 2, "WO": 1}


def xn_slot(s, b):
    return (b % 2, b % 2, 1, 0)[s - 1]


def hybrid_block_kernel(nc, x, Wqkv, bqkv, Wo, bo, wq, wk, wv, wo, qweight, scale, zero, bias, rope, out):
    steps = schedule()
    count, nth = {}, {}
    for st in steps:
        nth[st] = count.get(st[0], 0)
        count[st[0]] = nth[st] + 1
    bank_of, before, owner, turn, scores_on = {}, {}, [None] * BANKS, 0, False
    taken_by_scores = []
    for st in steps:
        if st[0] == "S" and not scores_on:
            scores_on, taken_by_scores = True, [o for o in owner[:6] if o]
        jobs = [(*st, j) for j in range(JOBS.get(st[0], 0))]
        jobs += [("VA", st[1], 0)] if st[0] == "SA" else []
        for job in jobs:
            turn += 1
            bank = 6 + turn % 2 if scores_on else turn % BANKS
            bank_of[job], before[job], owner[bank] = bank, owner[bank], job

    def job_count(job):
        if job[0] == "VA":
            return nth[("SA", job[1])] + 1
        return nth[job[:-1]] * JOBS[job[0]] + job[-1] + 1

    xt_slot, xt_before, xn_before, holder, xn_holder = {}, {}, {}, {}, {}
    for st in steps:
        if st[0] == "T":
            s, b = st[1:]
            slot = (b % 2, b % 2, 2, 0)[s - 1]
            xt_slot[st], xt_before[st] = slot, holder.get(slot)
            holder[slot] = {1: ("QKV", b, 1), 2: ("F", 2, b, 1, 0), 3: ("VP", 2 * b + 1, 0), 4: ("F", 4, b, 1, 0)}[s]
        if st[0] == "LN":
            s, b = st[1:]
            slot = xn_slot(s, b)
            xn_before[st] = xn_holder.get(slot)
            xn_holder[slot] = ("T", s, b, 1)

    def last_reader(job):
        return ("PROJ", job[1] * 2 + 1, 0) if job and job[0] == "VP" else job

    with ExitStack() as ctx:
        def sb(name, shape, dt, where=ctx):
            return where.enter_context(nc.sbuf_tensor(name, shape, dt))

        def sem(name):
            return ctx.enter_context(nc.semaphore(name))

        psum = ctx.enter_context(nc.psum_tensor("psum", [P, BANKS * BANK], F32))

        def bank(k, n=1):
            return psum[:, k * BANK:(k + n) * BANK]

        X = sb("X", [P, B, NT, C], F32)
        wf = sb("wf", [P, KT, C], F32R)
        scale_r = sb("scale_r", [P, C], F32)
        shift_r = sb("shift_r", [P, C], F32)
        row_sum = sb("row_sum", [P, 2, B, NT], F32)
        prod = sb("prod", [P, C], F32)
        wb_hi = sb("wb_hi", [P, 3, KT, C], F32R)
        wb_lo = sb("wb_lo", [P, 3, KT, C], F32R)
        wo_sb = sb("wo_sb", [P, KT, C], F32)
        XN = sb("XN", [P, 3, NT, C], F32)
        XT_hi = sb("XT_hi", [P, 3, KT, S], F32R)
        XT_lo = sb("XT_lo", [P, 3, KT, S], F32R)
        bias_f = sb("bias_f", [P, C], F32)
        ident = sb("ident", [P, P], F32)
        ident_h = sb("ident_h", [P, P], BF16)
        tri = sb("tri", [P, P], BF16)
        stats = sb("stats", [P, NT, 6], F32)
        mv = sb("mv", [P, NT, 2], F32)
        mhalf_var = sb("mhalf_var", [P, NT], F32)
        rstd = sb("rstd", [P, NT], F32)
        newton = sb("newton", [P, NT], F32)
        offset = sb("offset", [P, NT], F32)

        early = ExitStack()
        wqkv_hi = sb("wqkv_hi", [P, KT, 3 * DA], F32R, early)
        wqkv_lo = sb("wqkv_lo", [P, KT, 3 * DA], F32R, early)
        wo1 = sb("wo1", [P, C], F32, early)
        bias_o = sb("bias_o", [P, C], F32, early)
        bqkv_c = sb("bqkv_c", [P, 3], F32, early)
        stage = sb("stage", [P, 2, KT * C], F32, early)
        q_int = sb("q_int", [P, KT, C // 2], I32, early)
        zero_r = sb("zero_r", [P, C], F32, early)
        qkT = sb("qkT", [P, 2, 2, S], F32, early)
        vT = sb("vT", [P, 2, S], F32, early)
        va = sb("va", [P, 2, NT, DA], F32, early)
        EA = sb("EA", [P, 2, NT, S], F32, early)
        ETs = sb("ETs", [P, 2, NT, S], F32, early)
        OTa = sb("OTa", [P, 2, S], F32, early)
        nmax_a = sb("nmax_a", [P, 2, NT], F32, early)
        sum_a = sb("sum_a", [P, 2, NT], F32, early)
        inv_a = sb("inv_a", [P, 2, NT], F32, early)
        early.close()

        QS = sb("QS", [P, QK_SLOTS, UH, S], BF16)
        KS = sb("KS", [P, QK_SLOTS, UH, S], BF16)
        E = sb("E", [P, 2, GH * 3 * P], F32)
        V = sb("V", [P, V_SLOTS, NT, 2 * UH, 2 * HD], F32)
        parts = sb("parts", [P, 2, 3, 2 * S], BF16)
        SH = sb("SH", [P, 2, 2 * S], F32)
        CC = sb("CC", [P, 2, 2 * S], F32)
        OU = sb("OU", [P, 2, NG, S], F32)
        OT = sb("OT", [P, KT, S], F32)
        table = sb("table", [P, 2, S], F32)
        nmax = sb("nmax", [P, 2, NT, UH], F32)
        mrow = sb("mrow", [UH, 2, 2, S], BF16)
        inv_o = sb("inv_o", [P, NG * NT * GH], F32)

        scratch = nc.dram_tensor("qk_parts", (2, 3, 2, P, S), BF16, kind="Internal").ap()

        made = {k: sem(f"made_{k}") for k in [*JOBS, "VA", "S", "ST"]}
        x_loaded = [sem(f"x_loaded{b}") for b in range(B)]
        wqkv_loaded, small_loaded, q_loaded = sem("wqkv_loaded"), sem("small_loaded"), sem("q_loaded")
        wo1_loaded, wo_loaded, table_loaded = sem("wo1_loaded"), sem("wo_loaded"), sem("table_loaded")
        staged = [sem(f"staged{m}") for m in range(3)]
        consts_ready, consts_cleared = sem("consts_ready"), sem("consts_cleared")
        ones_ready = sem("ones_ready")
        wqkv_hi_ready, wqkv_lo_ready = sem("wqkv_hi_ready"), sem("wqkv_lo_ready")
        wf_ready, unpacked, stats_ready, row_shifted = sem("wf_ready"), sem("unpacked"), sem("stats_ready"), sem("row_shifted")
        wb_hi_ready, wb_lo_ready = sem("wb_hi_ready"), sem("wb_lo_ready")
        xn_ready, bias_added = sem("xn_ready"), sem("bias_added")
        xh_ready, xl_ready = sem("xh_ready"), sem("xl_ready")
        qkv_ready, va_ready, nmax_a_ready = sem("qkv_ready"), sem("va_ready"), sem("nmax_a_ready")
        ea_ready, ea_normed, et_ready, oa_ready = sem("ea_ready"), sem("ea_normed"), sem("et_ready"), sem("oa_ready")
        resid_a, resid_f, resid_o = sem("resid_a"), sem("resid_f"), sem("resid_o")
        rope_parts, roped = sem("rope_parts"), sem("roped")
        part1_ready, rest1_ready, part2_ready, part3_ready = sem("part1"), sem("rest1"), sem("part2"), sem("part3")
        v_ready, max_ready, m1_ready, m2_ready = sem("v_ready"), sem("max_ready"), sem("m1_ready"), sem("m2_ready")
        exp_ready, masked, ou_ready, o_ready, ot_ready = (sem("exp_ready"), sem("masked"), sem("ou_ready"),
                                                         sem("o_ready"), sem("ot_ready"))
        parts_stored = [sem(f"parts_stored{i}") for i in range(2)]
        qk_loaded = [sem(f"qk_loaded{i}") for i in range(QK_SLOTS)]
        m_loaded = [sem(f"m_loaded{i}") for i in range(2)]
        out_done = sem("out_done")
        dve_link, pool_link = sem("dve_link"), sem("pool_link")

        released = {"WT": wf_ready, "T": xl_ready, "QKV": qkv_ready, "VA": va_ready, "SA": ea_ready,
                    "ET": et_ready, "OA": oa_ready, "WA": resid_a, "F": resid_f, "PROJ": rope_parts,
                    "VP": v_ready, "MT": m2_ready, "PV": ou_ready, "NRM": o_ready, "DT": ot_ready,
                    "WO": resid_o}

        def wait_job(eng, job):
            eng.wait_ge(made[job[0]], job_count(job))

        def early_over(eng):
            eng.wait_ge(resid_a, B * NT)
            eng.wait_ge(wb_lo_ready, 3)
            eng.wait_ge(wf_ready, KT)

        bqkv_v = bqkv.rearrange("(j p) -> p j", p=P)
        x_v = x.rearrange("b (t p) n -> b p t n", p=P)
        out_v = out.rearrange("b (t p) n -> b p t n", p=P)

        def rows(w):
            return w.rearrange("(k p) n -> p k n", p=P)

        def staging(m):
            return stage[:, m % 2, :].rearrange("p (k n) -> p k n", k=KT)

        block = ctx.enter_context(nc.Block())

        @block.sync
        def _(sp):
            sp.dma_start(X[:, 0], x_v[0]).then_inc(x_loaded[0], 16)
            sp.dma_start(stage[:, 0, 0:KT * 3 * DA].rearrange("p (k n) -> p k n", k=KT),
                         rows(Wqkv)).then_inc(wqkv_loaded, 16)
            sp.dma_start(X[:, 1], x_v[1]).then_inc(x_loaded[1], 16)
            sp.dma_start(bqkv_c[:], bqkv_v, allow_slow_non_contiguous=True).then_inc(small_loaded, 16)
            sp.dma_start(scale_r[:], scale.rearrange("n a -> (n a)").partition_broadcast(P)).then_inc(small_loaded, 16)
            sp.dma_start(zero_r[:], zero.rearrange("n a -> (n a)").partition_broadcast(P)).then_inc(small_loaded, 16)
            sp.dma_start(bias_o[:], bo.partition_broadcast(P)).then_inc(small_loaded, 16)
            sp.dma_start(bias_f[:], bias.partition_broadcast(P)).then_inc(small_loaded, 16)
            sp.dma_start(q_int[:], rows(qweight)).then_inc(q_loaded, 16)
            sp.dma_start(wo1[:], Wo).then_inc(wo1_loaded, 16)
            sp.dma_start(X[:, 2], x_v[2]).then_inc(x_loaded[2], 16)
            sp.dma_start(X[:, 3], x_v[3]).then_inc(x_loaded[3], 16)
            sp.dma_start(wo_sb[:], rows(wo)).then_inc(wo_loaded, 16)
            for m, w in enumerate((wq, wk, wv)):
                if m == 0:
                    sp.wait_ge(unpacked, 1)
                elif m == 1:
                    sp.wait_ge(made["WT"], KT)
                else:
                    sp.wait_ge(wb_lo_ready, 1)
                sp.dma_start(staging(m), rows(w)).then_inc(staged[m], 16)
            early_over(sp)
            sp.dma_start(table[:], rope).then_inc(table_loaded, 16)
            for st in steps:
                if st[0] == "P3":
                    u = st[1]
                    sp.wait_ge(part3_ready, u + 1)
                    if u >= 2:
                        sp.wait_ge(qk_loaded[(u - 2) % QK_SLOTS], 16 * 2 * len(Q_PARTS) * ((u - 2) // QK_SLOTS + 1))
                    sp.dma_start(scratch[u % 2].rearrange("c a d t -> d (c a) t"),
                                 parts[:, u % 2].rearrange("p c (a t) -> p (c a) t", a=2)
                                 ).then_inc(parts_stored[u % 2], 16)
                    sp.wait_ge(parts_stored[u % 2], 16 * (u // 2 + 1))
                    if u >= QK_SLOTS:
                        sp.wait_ge(made["ST"], nth[("ST", u - QK_SLOTS, NG - 1)] + 1)
                    for a, (stack, which) in enumerate(((QS, Q_PARTS), (KS, K_PARTS))):
                        for row, c in enumerate(which):
                            sp.dma_start(stack[row * HD:(row + 1) * HD, u % QK_SLOTS],
                                         scratch[u % 2, c, a].rearrange("(h d) t -> d h t", d=HD)
                                         ).then_inc(qk_loaded[u % QK_SLOTS], 16)
                if st[0] == "MT":
                    u = st[1]
                    sp.wait_ge(m2_ready, nth[st] + 1)
                    sp.wait_ge(m1_ready, nth[st] + 1)
                    for r in range(2):
                        sp.dma_start(QS[KROWS + r:KROWS + r + 1, u % QK_SLOTS], mrow[:, u % 2, r]
                                     ).then_inc(m_loaded[u % 2], 16)
                if st[0] == "F" and st[1] == 4:
                    b, t = st[2:]
                    sp.wait_ge(resid_f, nth[st] + 1)
                    sp.dma_start(out_v[b][:, t], X[:, b, t]).then_inc(out_done, 16)
            sp.wait_ge(out_done, 16 * B * NT)

        @block.gpsimd
        def _(pool):
            links = [0]

            def link(ins):
                links[0] += 1
                ins.then_inc(pool_link, 1)
                pool.wait_ge(pool_link, links[0])

            nc.gpsimd.memset(ident[:], 0.0).then_inc(consts_cleared, 1)
            nc.gpsimd.memset(ident_h[:], 0.0).then_inc(consts_cleared, 1)
            nc.gpsimd.memset(tri[:], 0.0).then_inc(consts_cleared, 1)
            pool.wait_ge(consts_cleared, 3)
            for m in (ident, ident_h):
                nc.gpsimd.affine_select(out=m[:], in_=m[:], compare_op=ALU.not_equal, fill=1.0, base=0,
                                        pattern=[[-1, P]], channel_multiplier=1).then_inc(consts_ready, 1)
            nc.gpsimd.affine_select(out=tri[:], in_=tri[:], compare_op=ALU.is_ge, fill=MASKED, base=0,
                                    pattern=[[-1, P]], channel_multiplier=1).then_inc(consts_ready, 1)
            late, biases = False, 0
            for st in steps:
                if st[0] == "LN" and st[1] != 3:
                    biases += NT
                    s, b = st[1:]
                    pool.wait_ge(xn_ready, nth[st] + 1)
                    if s == 1 and b == 0:
                        pool.wait_ge(small_loaded, 16 * 5)
                    for t in range(NT):
                        nc.gpsimd.tensor_tensor(X[:, b, t], X[:, b, t], (bias_o if s == 1 else bias_f)[:], ALU.add
                                                ).then_inc(bias_added, 1)
                if st[0] == "WB":
                    m = st[1]
                    pool.wait_ge(staged[m], 16)
                    pool.wait_ge(wb_hi_ready, m + 1)
                    nc.gpsimd.tensor_tensor(wb_lo[:, m], staging(m), wb_hi[:, m].bitcast(F32), ALU.subtract
                                            ).then_inc(wb_lo_ready, 1)
                if st[0] == "PROJ":
                    u = st[1]
                    if not late:
                        late = True
                        early_over(pool)
                        pool.wait_ge(bias_added, biases)
                        nc.gpsimd.memset(KS[KROWS:P], 1.0).then_inc(ones_ready, 1)
                        pool.wait_ge(ones_ready, 1)
                        nc.gpsimd.memset(V[:], 1.0).then_inc(ones_ready, 1)
                        pool.wait_ge(table_loaded, 16)
                    pool.wait_ge(rope_parts, u + 1)
                    sh = SH[:, u % 2].rearrange("p (a t) -> p a t", a=2)
                    link(nc.gpsimd.tensor_tensor(sh, sh, table[:, 1:2, :].to_broadcast((P, 2, S)), ALU.mult))
                    nc.gpsimd.tensor_tensor(SH[:, u % 2], SH[:, u % 2], CC[:, u % 2], ALU.add).then_inc(roped, 1)
                if st[0] == "P1":
                    u = st[1]
                    pool.wait_ge(roped, u + 1)
                    pool.wait_ge(part1_ready, u + 1)
                    nc.gpsimd.tensor_tensor(SH[:, u % 2], SH[:, u % 2], parts[:, u % 2, 0], ALU.subtract
                                            ).then_inc(rest1_ready, 1)
                if st[0] == "ST":
                    n = nth[st]
                    pool.wait_ge(exp_ready, n + 1)
                    for at, width in ((0, S), (GH * S, P)):
                        e = E[:, n % 2, at:at + GH * width].rearrange("p (h q) -> p h q", h=GH)[:, :, 0:P]
                        last = nc.gpsimd.affine_select(out=e, in_=e, compare_op=ALU.is_ge, fill=0.0, base=0,
                                                       pattern=[[0, GH], [1, P]], channel_multiplier=-1)
                    last.then_inc(masked, 1)

        @block.scalar
        def _(act):
            late = False

            def copy(out_, in_):
                return nc.scalar.activation(out_, in_, ACT.Copy)

            for st in steps:
                k = st[0]
                if k == "WQ":
                    act.wait_ge(wqkv_loaded, 16)
                    copy(wqkv_hi[:].rearrange("p k n -> p (k n)"), stage[:, 0, 0:KT * 3 * DA]
                         ).then_inc(wqkv_hi_ready, 1)
                elif k == "WB":
                    m = st[1]
                    act.wait_ge(staged[m], 16)
                    copy(wb_hi[:, m], staging(m)).then_inc(wb_hi_ready, 1)
                elif k == "WT":
                    wait_job(act, (*st, 0))
                    copy(wf[:, st[1]], bank(bank_of[(*st, 0)])).then_inc(wf_ready, 1)
                elif k == "LN":
                    s, b = st[1:]
                    act.wait_ge(stats_ready, nth[st] + 1)
                    if xn_before[st]:
                        wait_job(act, xn_before[st])
                    for t in range(NT):
                        more = {"accum_out": row_sum[:, s // 2 - 1, b, t:t + 1]} if s in (2, 4) else {}
                        last = nc.scalar.activation(XN[:, xn_slot(s, b), t], X[:, b, t], ACT.Identity,
                                                    bias=offset[:, t:t + 1], scale=rstd[:, t:t + 1], **more)
                    last.then_inc(xn_ready, 1)
                elif k == "T":
                    slot = xt_slot[st]
                    for j in range(2):
                        wait_job(act, (*st, j))
                        if j == 0 and xt_before[st]:
                            wait_job(act, last_reader(xt_before[st]))
                        copy(XT_hi[:, slot, 2 * j:2 * j + 2].rearrange("p k n -> p (k n)"),
                             bank(bank_of[(*st, j)])).then_inc(xh_ready, 1)
                elif k == "QKV":
                    b = st[1]
                    wait_job(act, (*st, 0))
                    if b == 0:
                        act.wait_ge(small_loaded, 16 * 5)
                    if b >= 2:
                        wait_job(act, ("SA", b - 2, 0))
                    ps = bank(bank_of[(*st, 0)])
                    nc.scalar.activation(qkT[:, b % 2, 0], ps[:, 0:S], ACT.Identity, bias=bqkv_c[:, 0:1])
                    nc.scalar.activation(qkT[:, b % 2, 1], ps[:, S:2 * S], ACT.Identity, bias=bqkv_c[:, 1:2]
                                         ).then_inc(qkv_ready, 1)
                    wait_job(act, (*st, 1))
                    if b >= 2:
                        wait_job(act, ("VA", b - 2, 0))
                    nc.scalar.activation(vT[:, b % 2], bank(bank_of[(*st, 1)])[:, 0:S], ACT.Identity,
                                         bias=bqkv_c[:, 2:3]).then_inc(qkv_ready, 1)
                elif k == "SA":
                    b = st[1]
                    wait_job(act, ("VA", b, 0))
                    if b >= 2:
                        wait_job(act, ("OA", b - 2, 0))
                    copy(va[:, b % 2].rearrange("p t d -> p (t d)"), bank(bank_of[("VA", b, 0)])[:, 0:NT * DA]
                         ).then_inc(va_ready, 1)
                elif k == "SM":
                    b = st[1]
                    act.wait_ge(nmax_a_ready, b + 1)
                    if b >= 2:
                        wait_job(act, ("ET", b - 2, 0))
                    ps = bank(bank_of[("SA", b, 0)])
                    for t in range(NT):
                        last = nc.scalar.activation(EA[:, b % 2, t], ps[:, t * S:(t + 1) * S], ACT.Exp,
                                                    bias=nmax_a[:, b % 2, t:t + 1], scale=float(DA) ** -0.5,
                                                    accum_out=sum_a[:, b % 2, t:t + 1])
                    last.then_inc(ea_ready, 1)
                elif k == "ET":
                    b = st[1]
                    wait_job(act, (*st, 0))
                    if b >= 2:
                        wait_job(act, ("OA", b - 2, 0))
                    copy(ETs[:, b % 2].rearrange("p k q -> p (k q)"), bank(bank_of[(*st, 0)])).then_inc(et_ready, 1)
                elif k == "OA":
                    b = st[1]
                    wait_job(act, (*st, 0))
                    if b >= 2:
                        wait_job(act, ("WA", b - 2, NT - 1))
                    copy(OTa[:, b % 2], bank(bank_of[(*st, 0)])[:, 0:S]).then_inc(oa_ready, 1)
                elif k == "P1":
                    u = st[1]
                    if not late:
                        late = True
                        early_over(act)
                    act.wait_ge(roped, u + 1)
                    if u >= 2:
                        act.wait_ge(parts_stored[u % 2], 16 * (u // 2))
                    copy(parts[:, u % 2, 0], SH[:, u % 2]).then_inc(part1_ready, 1)
                elif k == "P2":
                    u = st[1]
                    act.wait_ge(rest1_ready, u + 1)
                    copy(parts[:, u % 2, 1], SH[:, u % 2]).then_inc(part2_ready, 1)
                elif k == "VP":
                    v = st[1]
                    wait_job(act, (*st, 0))
                    if v == 0:
                        act.wait_ge(ones_ready, 2)
                    if v >= V_SLOTS:
                        wait_job(act, ("PV", 2 * (v - V_SLOTS) + 1, NG - 1, 0))
                    copy(V[:, v % V_SLOTS, :, :, 0:HD],
                         bank(bank_of[(*st, 0)]).rearrange("p (t h d) -> p t h d", t=NT, d=HD)).then_inc(v_ready, 1)
                elif k == "MT":
                    u = st[1]
                    wait_job(act, (*st, 0))
                    if u >= 2:
                        act.wait_ge(m_loaded[u % 2], 32 * (u // 2))
                    copy(mrow[:, u % 2, 0], bank(bank_of[(*st, 0)])[0:UH, 0:S]).then_inc(m1_ready, 1)
                elif k == "ST":
                    n = nth[st]
                    act.wait_ge(made["ST"], n + 1)
                    if n >= 2:
                        wait_job(act, ("PV", *divmod(n - 2, NG), 0))
                    nc.scalar.activation(E[:, n % 2], bank(3, 3), ACT.Exp, scale=float(HD) ** -0.5
                                         ).then_inc(exp_ready, 1)
                elif k == "PV":
                    u, g = st[1:]
                    wait_job(act, (*st, 0))
                    if u >= 2:
                        wait_job(act, ("NRM", u - 2, 0))
                    copy(OU[:, u % 2, g], bank(bank_of[(*st, 0)])[:, 0:S]).then_inc(ou_ready, 1)
                elif k == "DT":
                    b = st[1]
                    for j in range(2):
                        wait_job(act, (*st, j))
                        if b and j == 0:
                            wait_job(act, ("WO", b - 1, NT - 1, 0))
                        copy(OT[:, 2 * j:2 * j + 2].rearrange("p k n -> p (k n)"), bank(bank_of[(*st, j)])
                             ).then_inc(ot_ready, 1)

        @block.vector
        def _(dve):
            links = [0]
            late = False
            bias_n = {}
            for st in steps:
                if st[0] == "LN" and st[1] != 3:
                    bias_n[st[1:]] = (len(bias_n) + 1) * NT

            def link(ins):
                links[0] += 1
                ins.then_inc(dve_link, 1)
                dve.wait_ge(dve_link, links[0])

            def add_residual(job, b, t, sem_):
                wait_job(dve, job)
                nc.vector.tensor_tensor(X[:, b, t], X[:, b, t], bank(bank_of[job]), ALU.add).then_inc(sem_, 1)

            for st in steps:
                k = st[0]
                if k == "WQ":
                    dve.wait_ge(wqkv_loaded, 16)
                    dve.wait_ge(wqkv_hi_ready, 1)
                    nc.vector.tensor_tensor(wqkv_lo[:].rearrange("p k n -> p (k n)"), stage[:, 0, 0:KT * 3 * DA],
                                            wqkv_hi[:].bitcast(F32).rearrange("p k n -> p (k n)"), ALU.subtract
                                            ).then_inc(wqkv_lo_ready, 1)
                elif k == "DQ":
                    dve.wait_ge(q_loaded, 16)
                    dve.wait_ge(wqkv_lo_ready, 1)
                    w_int = stage[:, 0, :].bitcast(I32).rearrange("p (k n) -> p k n", k=KT)
                    w = stage[:, 0, :].bitcast(I32).rearrange("p (j i e) -> p j i e", j=KT, e=2)
                    nc.vector.tensor_scalar(w[:, :, :, 0], q_int[:], 4, 15, ALU.logical_shift_right, ALU.bitwise_and)
                    link(nc.vector.tensor_scalar(w[:, :, :, 1], q_int[:], 15, None, ALU.bitwise_and))
                    nc.vector.tensor_copy(staging(1), w_int).then_inc(unpacked, 1)
                    dve.wait_ge(small_loaded, 16 * 5)
                    link(nc.vector.scalar_tensor_tensor(shift_r[:], zero_r[:], -1.0, scale_r[:], ALU.mult, ALU.mult))
                elif k == "LN":
                    s, b = st[1:]
                    slot = xn_slot(s, b)
                    if s == 1:
                        dve.wait_ge(x_loaded[b], 16)
                    elif s == 2:
                        dve.wait_ge(resid_a, (b + 1) * NT)
                    elif s == 3:
                        dve.wait_ge(resid_f, nth[("F", 2, b, NT - 1)] + 1)
                    else:
                        dve.wait_ge(resid_o, (b + 1) * NT)
                    if nth[st]:
                        dve.wait_ge(xn_ready, nth[st])
                    nc.vector.bn_stats(stats[:, 0], X[:, b, 0])
                    link(nc.vector.bn_stats(stats[:, 1], X[:, b, 1]))
                    nc.vector.bn_aggr(mv[:, 0], stats[:, 0])
                    link(nc.vector.bn_aggr(mv[:, 1], stats[:, 1]))
                    link(nc.vector.tensor_scalar(mhalf_var[:], mv[:, :, 1], EPS, -0.5, ALU.add, ALU.mult))
                    link(nc.vector.tensor_scalar(rstd[:].bitcast(I32), mhalf_var[:].bitcast(I32), -0.5, RSQRT_MAGIC,
                                                 ALU.mult, ALU.add))
                    for _ in range(3):
                        for t in range(NT):
                            last = nc.vector.scalar_tensor_tensor(newton[:, t:t + 1], rstd[:, t:t + 1],
                                                                  mhalf_var[:, t:t + 1], rstd[:, t:t + 1],
                                                                  ALU.mult, ALU.mult)
                        link(last)
                        link(nc.vector.scalar_tensor_tensor(rstd[:], newton[:], 1.5, rstd[:], ALU.add, ALU.mult))
                    nc.vector.scalar_tensor_tensor(offset[:], mv[:, :, 0], -1.0, rstd[:], ALU.mult, ALU.mult
                                                   ).then_inc(stats_ready, 1)
                elif k == "T":
                    slot = xt_slot[st]
                    for j in range(2):
                        dve.wait_ge(xh_ready, nth[st] * 2 + j + 1)
                        if j == 0 and xt_before[st]:
                            wait_job(dve, last_reader(xt_before[st]))
                        nc.vector.tensor_tensor(XT_lo[:, slot, 2 * j:2 * j + 2].rearrange("p k n -> p (k n)"),
                                                bank(bank_of[(*st, j)]),
                                                XT_hi[:, slot, 2 * j:2 * j + 2].bitcast(F32).rearrange("p k n -> p (k n)"),
                                                ALU.subtract).then_inc(xl_ready, 1)
                elif k == "SA":
                    b = st[1]
                    wait_job(dve, (*st, 0))
                    if b >= 2:
                        dve.wait_ge(ea_ready, b - 1)
                    link(nc.vector.tensor_reduce(nmax_a[:, b % 2], bank(bank_of[(*st, 0)]).rearrange(
                        "p (t k) -> p t k", t=NT), AX, ALU.max))
                    nc.vector.tensor_scalar(nmax_a[:, b % 2], nmax_a[:, b % 2], -float(DA) ** -0.5, None, ALU.mult
                                            ).then_inc(nmax_a_ready, 1)
                elif k == "SM":
                    b = st[1]
                    dve.wait_ge(ea_ready, b + 1)
                    link(nc.vector.reciprocal(inv_a[:, b % 2], sum_a[:, b % 2]))
                    for t in range(NT):
                        last = nc.vector.tensor_scalar(EA[:, b % 2, t], EA[:, b % 2, t], inv_a[:, b % 2, t:t + 1], None,
                                                       ALU.mult)
                    last.then_inc(ea_normed, 1)
                elif k == "WA":
                    b = st[1]
                    dve.wait_ge(bias_added, bias_n[(1, b)])
                    for t in range(NT):
                        add_residual((*st, t), b, t, resid_a)
                elif k == "F":
                    sn, b, t = st[1:]
                    dve.wait_ge(bias_added, bias_n[(sn, b)])
                    nc.vector.scalar_tensor_tensor(X[:, b, t], shift_r[:], row_sum[:, sn // 2 - 1, b, t:t + 1],
                                                   X[:, b, t], ALU.mult, ALU.add).then_inc(row_shifted, 1)
                    if nth[st]:
                        dve.wait_ge(resid_f, nth[st])
                    wait_job(dve, (*st, 0))
                    link(nc.vector.tensor_tensor(prod[:], bank(bank_of[(*st, 0)]), scale_r[:], ALU.mult))
                    dve.wait_ge(row_shifted, nth[st] + 1)
                    nc.vector.tensor_tensor(X[:, b, t], X[:, b, t], prod[:], ALU.add).then_inc(resid_f, 1)
                elif k == "WO":
                    add_residual((*st, 0), st[1], st[2], resid_o)
                elif k == "PROJ":
                    u = st[1]
                    if not late:
                        late = True
                        early_over(dve)
                        dve.wait_ge(table_loaded, 16)
                    wait_job(dve, (*st, 0))
                    if u >= 2:
                        dve.wait_ge(part3_ready, u - 1)
                        dve.wait_ge(roped, u - 1)
                    ps = bank(bank_of[(*st, 0)])
                    nc.vector.stream_shuffle(SH[:, u % 2], ps, [i ^ 1 for i in range(32)])
                    nc.vector.tensor_tensor(CC[:, u % 2].rearrange("p (a t) -> p a t", a=2),
                                            ps.rearrange("p (a t) -> p a t", a=2),
                                            table[:, 0:1, :].to_broadcast((P, 2, S)), ALU.mult
                                            ).then_inc(rope_parts, 1)
                elif k == "P3":
                    u = st[1]
                    dve.wait_ge(part2_ready, u + 1)
                    nc.vector.tensor_tensor(parts[:, u % 2, 2], SH[:, u % 2], parts[:, u % 2, 1], ALU.subtract
                                            ).then_inc(part3_ready, 1)
                elif k == "S":
                    u, g = st[1:]
                    dve.wait_ge(made["S"], nth[st] + 1)
                    if g == 0 and u >= 2:
                        wait_job(dve, ("MT", u - 2, 0))
                    nc.vector.tensor_reduce(nmax[:, u % 2, 0, g * GH:(g + 1) * GH],
                                            bank(0).rearrange("p (h k) -> p h k", h=GH), AX, ALU.max, negate=True)
                    nc.vector.tensor_reduce(nmax[:, u % 2, 1, g * GH:(g + 1) * GH],
                                            bank(1, 2).rearrange("p (h k) -> p h k", h=GH), AX, ALU.max, negate=True
                                            ).then_inc(max_ready, 1)
                elif k == "MT":
                    u = st[1]
                    dve.wait_ge(m1_ready, nth[st] + 1)
                    nc.vector.tensor_tensor(mrow[:, u % 2, 1], bank(bank_of[(*st, 0)])[0:UH, 0:S], mrow[:, u % 2, 0],
                                            ALU.subtract).then_inc(m2_ready, 1)
                elif k == "NRM":
                    u = st[1]
                    b, m = divmod(u, KT)
                    wait_job(dve, (*st, 0))
                    ps = bank(bank_of[(*st, 0)]).rearrange("p (g t h d) -> p g t h d", g=NG, t=NT, h=GH)
                    inv = inv_o[:].rearrange("p (g t h) -> p g t h", g=NG, t=NT)
                    link(nc.vector.reciprocal(inv, ps[:, :, :, :, HD]))
                    if m == 0 and b:
                        wait_job(dve, ("DT", b - 1, 1))
                    for t in range(NT):
                        o = XN[:, 2, t, m * P:(m + 1) * P].rearrange("p (g h d) -> p g h d", g=NG, h=GH)
                        last = nc.vector.tensor_tensor(
                            o, ps[:, :, t, :, 0:HD],
                            inv[:, :, t, :].unsqueeze(3).to_broadcast((P, NG, GH, HD)), ALU.mult)
                    last.then_inc(o_ready, 1)

        @block.tensor
        def _(pe):
            def take(job):
                if before[job]:
                    pe.wait_ge(released[before[job][0]], job_count(before[job]))
                return bank(bank_of[job])

            def three_pass(out_, stat, mov, first, last):
                nc.tensor.matmul(out_, stat[0], mov[1], start=first, stop=False)
                nc.tensor.matmul(out_, stat[1], mov[0], start=False, stop=False)
                return nc.tensor.matmul(out_, stat[0], mov[0], start=False, stop=last)

            scores_on = False
            for st in steps:
                k = st[0]
                if k == "WT":
                    if st[1] == 0:
                        pe.wait_ge(unpacked, 1)
                        pe.wait_ge(consts_ready, 3)
                    ps = take((*st, 0))
                    for j in range(KT):
                        last = nc.tensor.transpose(ps[:, j * P:(j + 1) * P],
                                                   staging(1)[:, j, st[1] * P:(st[1] + 1) * P], ident[:])
                    last.then_inc(made[k], 1)
                elif k == "T":
                    s, b = st[1:]
                    slot = xn_slot(s, b)
                    if nth[st] == 0:
                        pe.wait_ge(consts_ready, 3)
                    pe.wait_ge(xn_ready, nth[("LN", s, b)] + 1)
                    for j in range(2):
                        ps = take((*st, j))
                        for kk in range(2):
                            for t in range(NT):
                                c = (2 * j + kk) * P
                                last = nc.tensor.transpose(ps[:, kk * S + t * P:kk * S + (t + 1) * P],
                                                           XN[:, slot, t, c:c + P], ident[:])
                        last.then_inc(made[k], 1)
                elif k == "QKV":
                    b = st[1]
                    pe.wait_ge(xl_ready, (nth[("T", 1, b)] + 1) * 2)
                    pe.wait_ge(xh_ready, (nth[("T", 1, b)] + 1) * 2)
                    pe.wait_ge(wqkv_lo_ready, 1)
                    for j, blocks in enumerate(((0, 1), (2,))):
                        ps = take((*st, j))
                        for i, m in enumerate(blocks):
                            for kt in range(KT):
                                last = three_pass(ps[:, i * S:(i + 1) * S],
                                                  [w[:, kt, m * DA:(m + 1) * DA] for w in (wqkv_hi, wqkv_lo)],
                                                  [xt[:, b % 2, kt] for xt in (XT_hi, XT_lo)],
                                                  kt == 0, kt == KT - 1)
                        last.then_inc(made[k], 1)
                elif k == "SA":
                    b = st[1]
                    pe.wait_ge(qkv_ready, 2 * (b + 1))
                    ps = take((*st, 0))
                    for t in range(NT):
                        last = nc.tensor.matmul(ps[:, t * S:(t + 1) * S], qkT[:, b % 2, 0, t * P:(t + 1) * P],
                                                qkT[:, b % 2, 1], start=True, stop=True)
                    last.then_inc(made[k], 1)
                    ps = take(("VA", b, 0))
                    for t in range(NT):
                        last = nc.tensor.transpose(ps[:, t * DA:(t + 1) * DA], vT[:, b % 2, t * P:(t + 1) * P], ident[:])
                    last.then_inc(made["VA"], 1)
                elif k == "ET":
                    b = st[1]
                    pe.wait_ge(ea_normed, b + 1)
                    ps = take((*st, 0))
                    for kt in range(NT):
                        for t in range(NT):
                            last = nc.tensor.transpose(ps[:, kt * S + t * P:kt * S + (t + 1) * P],
                                                       EA[:, b % 2, t, kt * P:(kt + 1) * P], ident[:])
                    last.then_inc(made[k], 1)
                elif k == "OA":
                    b = st[1]
                    pe.wait_ge(et_ready, b + 1)
                    pe.wait_ge(va_ready, b + 1)
                    ps = take((*st, 0))
                    for kt in range(NT):
                        last = nc.tensor.matmul(ps[:, 0:S], va[:, b % 2, kt], ETs[:, b % 2, kt],
                                                start=kt == 0, stop=kt == NT - 1)
                    last.then_inc(made[k], 1)
                elif k == "WA":
                    b = st[1]
                    pe.wait_ge(oa_ready, b + 1)
                    if b == 0:
                        pe.wait_ge(wo1_loaded, 16)
                    for t in range(NT):
                        ps = take((*st, t))
                        nc.tensor.matmul(ps, OTa[:, b % 2, t * P:(t + 1) * P], wo1[:], start=True, stop=True
                                         ).then_inc(made[k], 1)
                elif k == "F":
                    s, b, t = st[1:]
                    tn = nth[("T", s, b)]
                    slot = xt_slot[("T", s, b)]
                    pe.wait_ge(xl_ready, (tn + 1) * 2)
                    pe.wait_ge(xh_ready, (tn + 1) * 2)
                    pe.wait_ge(wf_ready, KT)
                    ps = take((*st, 0))
                    for kt in range(KT):
                        tok = slice(t * P, (t + 1) * P)
                        nc.tensor.matmul(ps, XT_lo[:, slot, kt, tok], wf[:, kt], start=kt == 0, stop=False)
                        last = nc.tensor.matmul(ps, XT_hi[:, slot, kt, tok], wf[:, kt], start=False,
                                                stop=kt == KT - 1)
                    last.then_inc(made[k], 1)
                elif k == "PROJ":
                    u = st[1]
                    b, m = divmod(u, KT)
                    pe.wait_ge(xl_ready, (nth[("T", 3, b)] + 1) * 2)
                    pe.wait_ge(xh_ready, (nth[("T", 3, b)] + 1) * 2)
                    if u == 0:
                        pe.wait_ge(wb_hi_ready, 3)
                        pe.wait_ge(wb_lo_ready, 3)
                    ps = take((*st, 0))
                    for a in range(2):
                        for kt in range(KT):
                            last = three_pass(ps[:, a * S:(a + 1) * S],
                                              [w[:, a, kt, m * P:(m + 1) * P] for w in (wb_hi, wb_lo)],
                                              [xt[:, 2, kt] for xt in (XT_hi, XT_lo)], kt == 0, kt == KT - 1)
                    last.then_inc(made[k], 1)
                elif k == "VP":
                    m = st[1] % 2
                    ps = take((*st, 0))
                    for t in range(NT):
                        for kt in range(KT):
                            last = three_pass(ps[:, t * S:(t + 1) * S],
                                              [xt[:, 2, kt, t * P:(t + 1) * P] for xt in (XT_hi, XT_lo)],
                                              [w[:, 2, kt, m * S:(m + 1) * S] for w in (wb_hi, wb_lo)],
                                              kt == 0, kt == KT - 1)
                    last.then_inc(made[k], 1)
                elif k == "S":
                    u, g = st[1:]
                    slot = u % QK_SLOTS
                    pe.wait_ge(qk_loaded[slot], 16 * 2 * len(Q_PARTS) * (u // QK_SLOTS + 1))
                    if not scores_on:
                        scores_on = True
                        for job in taken_by_scores:
                            pe.wait_ge(released[job[0]], job_count(job))
                    if nth[st]:
                        pe.wait_ge(max_ready, nth[st])
                    nc.tensor.matmul(bank(0).rearrange("p (h k) -> p h k", h=GH), ident_h[:],
                                     tri[:].unsqueeze(1).to_broadcast((P, GH, P)),
                                     start=True, stop=False, skip_group_check=True)
                    for half in range(2):
                        nc.tensor.matmul(bank(1 + half).rearrange("p (h k) -> p h k", h=2)[:, :, P:S], ident_h[:],
                                         tri[:].unsqueeze(1).to_broadcast((P, 2, P)),
                                         start=True, stop=False, skip_group_check=True)
                    for j in range(GH):
                        h = g * GH + j
                        nc.tensor.matmul(bank(0)[:, j * P:(j + 1) * P], QS[0:KROWS, slot, h, 0:P],
                                         KS[0:KROWS, slot, h, 0:P], start=False, stop=True, skip_group_check=True)
                        last = nc.tensor.matmul(bank(1, 2)[:, j * S:(j + 1) * S], QS[0:KROWS, slot, h, P:S],
                                                KS[0:KROWS, slot, h, :], start=False, stop=True, skip_group_check=True)
                    last.then_inc(made[k], 1)
                elif k == "MT":
                    u = st[1]
                    pe.wait_ge(max_ready, nth[("S", u, NG - 1)] + 1)
                    ps = take((*st, 0))
                    for t in range(NT):
                        last = nc.tensor.transpose(ps[0:UH, t * P:(t + 1) * P], nmax[:, u % 2, t], ident[:])
                    last.then_inc(made[k], 1)
                elif k == "ST":
                    u, g = st[1:]
                    slot = u % QK_SLOTS
                    if g == 0:
                        pe.wait_ge(m_loaded[u % 2], 32 * (u // 2 + 1))
                    if u == 0 and g == 0:
                        pe.wait_ge(ones_ready, 2)
                    if nth[st]:
                        pe.wait_ge(exp_ready, nth[st])
                    for j in range(GH):
                        h = g * GH + j
                        nc.tensor.matmul(bank(3, 2)[:, j * S:(j + 1) * S], KS[0:SROWS, slot, h, 0:P],
                                         QS[0:SROWS, slot, h, :], start=True, stop=True)
                        last = nc.tensor.matmul(bank(5)[:, j * P:(j + 1) * P], KS[0:SROWS, slot, h, P:S],
                                                QS[0:SROWS, slot, h, P:S], start=True, stop=True)
                    last.then_inc(made[k], 1)
                elif k == "PV":
                    u, g = st[1:]
                    n = u * NG + g
                    pe.wait_ge(masked, n + 1)
                    pe.wait_ge(v_ready, u // 2 + 1)
                    ps = take((*st, 0))
                    for kt in range(NT):
                        for j in range(GH):
                            v = V[:, (u // 2) % V_SLOTS, kt, (u % 2) * UH + g * GH + j]
                            at = j * S if kt == 0 else GH * S + j * P
                            last = nc.tensor.matmul(ps[j * 32:(j + 1) * 32, kt * P:S], v,
                                                    E[:, n % 2, at:at + S - kt * P],
                                                    start=kt == 0, stop=kt == NT - 1, skip_group_check=True)
                    last.then_inc(made[k], 1)
                elif k == "NRM":
                    u = st[1]
                    pe.wait_ge(ou_ready, (u + 1) * NG)
                    ps = take((*st, 0))
                    for g in range(NG):
                        for t in range(NT):
                            c = (g * NT + t) * P
                            last = nc.tensor.transpose(ps[:, c:c + P], OU[:, u % 2, g, t * P:(t + 1) * P], ident[:])
                    last.then_inc(made[k], 1)
                elif k == "DT":
                    b = st[1]
                    pe.wait_ge(o_ready, (b + 1) * KT)
                    for j in range(2):
                        ps = take((*st, j))
                        for kk in range(2):
                            for t in range(NT):
                                c = (2 * j + kk) * P
                                last = nc.tensor.transpose(ps[:, kk * S + t * P:kk * S + (t + 1) * P],
                                                           XN[:, 2, t, c:c + P], ident[:])
                        last.then_inc(made[k], 1)
                elif k == "WO":
                    b, t = st[1:]
                    pe.wait_ge(ot_ready, (b + 1) * 2)
                    if b == 0:
                        pe.wait_ge(wo_loaded, 16)
                    ps = take((*st, 0))
                    for kt in range(KT):
                        last = nc.tensor.matmul(ps, OT[:, kt, t * P:(t + 1) * P], wo_sb[:, kt],
                                                start=kt == 0, stop=kt == KT - 1)
                    last.then_inc(made[k], 1)


_INS = ["L0_attn_a_x", "L0_attn_a_Wqkv", "L0_attn_a_bqkv", "L0_attn_a_Wo", "L0_attn_a_bo", "L0_attn_b_wq",
        "L0_attn_b_wk", "L0_attn_b_wv", "L0_attn_b_wo", "L0_ffn_qweight", "L0_ffn_scale", "L0_ffn_zero",
        "L0_ffn_bias"]


def kernel(**inputs):
    import concourse.bacc as bacc
    from concourse.bass_utils import run_bass_kernel_spmd

    nc = bacc.Bacc("TRN2", target_bir_lowering=False, num_devices=1)
    arrays = {n: np.ascontiguousarray(inputs[n]) for n in _INS}
    arrays["rope_table"] = rope_tables()
    args = [nc.dram_tensor(n, a.shape, mybir.dt.from_np(a.dtype), kind="ExternalInput").ap()
            for n, a in arrays.items()]
    out = nc.dram_tensor("out", (B, S, C), F32, kind="ExternalOutput").ap()
    hybrid_block_kernel(nc, *args, out)
    r = run_bass_kernel_spmd(nc, [arrays], core_ids=[0])
    return r.results[0]["out"]
```

```python
from contextlib import ExitStack

import numpy as np

import concourse.bass as bass
from concourse import mybir

F32 = mybir.dt.float32
F32R = mybir.dt.float32r
BF16 = mybir.dt.bfloat16
I32 = mybir.dt.int32
ALU = mybir.AluOpType
ACT = mybir.ActivationFunctionType
AX = mybir.AxisListType.X

P = 128
B, S, C = 4, 256, 512
NT = S // P
KT = C // P
DA = C // 4
H, HD = 32, 16
THETA = 10000.0
EPS = 1e-5
UH = P // HD
NU = B * KT
GH = 4
NG = UH // GH
Q_PARTS = (0, 0, 0, 1, 1, 2)
K_PARTS = (0, 1, 2, 0, 1, 0)
KROWS = HD * len(Q_PARTS)
SROWS = KROWS + 2
QK_SLOTS = 4
V_SLOTS = 3
MASKED = -1.0e30
TWO_ONES = float(np.uint32(0x3F803F80).view(np.float32))
RSQRT_MAGIC = float(0x5F3759DF - (1 << 30) - (1 << 22))
NEWTON = 3
STAT_LINKS = 5 + 2 * NEWTON
STAT_SLOTS = 2
STAT_PARTS = (range(0, 3), range(3, 6), range(6, 9), range(9, STAT_LINKS))
BANKS = 8
BANK = 512


def rope_tables():
    inv = 1.0 / THETA ** (np.arange(0, HD, 2)[:HD // 2].astype(np.float32) / HD)
    f = np.outer(np.arange(S), inv).astype(np.float32)
    pair = (np.arange(P) % HD) // 2
    sign = np.where(np.arange(P) % 2 == 0, -1.0, 1.0).astype(np.float32)
    cos = np.cos(f).T[pair]
    sin = np.sin(f).T[pair] * sign[:, None]
    return np.ascontiguousarray(np.stack([cos, sin], 1).astype(np.float32))


PROLOGUE = [
    ("LN", 1, 0, 0), ("WQ",), ("KEEP", 0, 20), ("LN", 1, 0, 1), ("LN", 1, 0, 2), ("LN", 1, 0, 3),
    ("LN", 1, 1, 0), ("LN", 1, 1, 1), ("LN", 1, 1, 2), ("LN", 1, 1, 3), ("NORM", 1, 0), ("T", 1, 0),
    ("NORM", 1, 1), ("DQ",), ("LN", 1, 2, 0), ("T", 1, 1), ("QKV", 0), ("WT", 0), ("WT", 1), ("LN", 1, 2, 1),
    ("LN", 1, 2, 2), ("SA", 0), ("LN", 1, 2, 3), ("SM", 0), ("NORM", 1, 2), ("WB", 0, 0), ("QKV", 1),
    ("ET", 0), ("T", 1, 2), ("LN", 1, 3, 0), ("WT", 2), ("SA", 1), ("WB", 0, 1), ("LN", 1, 3, 1), ("WT", 3),
    ("SM", 1), ("OA", 0), ("QKV", 2), ("LN", 1, 3, 2), ("LN", 1, 3, 3), ("NORM", 1, 3), ("WB", 1, 0),
    ("ET", 1), ("WA", 0), ("LN", 2, 0, 0), ("LN", 2, 0, 1), ("LN", 2, 0, 2), ("SA", 2), ("OA", 1),
    ("WB", 1, 1), ("LN", 2, 0, 3), ("WA", 1), ("WB", 2, 0), ("SM", 2), ("LN", 2, 1, 0), ("T", 1, 3),
    ("NORM", 2, 0), ("T", 2, 0), ("LN", 2, 1, 1), ("LN", 2, 1, 2), ("LN", 2, 1, 3), ("WB", 2, 1), ("ET", 2),
    ("F", 2, 0, 1), ("NORM", 2, 1), ("F", 2, 0, 0), ("LN", 3, 0, 0), ("LN", 3, 0, 1), ("QKV", 3),
    ("LN", 3, 0, 2), ("T", 2, 1), ("OA", 2), ("SA", 3), ("LN", 3, 0, 3), ("F", 2, 1, 1), ("WA", 2),
    ("NORM", 3, 0), ("SM", 3), ("F", 2, 1, 0), ("ET", 3), ("T", 3, 0), ("OA", 3), ("WA", 3), ("WB", 3, 0),
    ("LN", 2, 2, 0), ("LN", 2, 2, 1), ("LN", 2, 2, 2), ("LN", 2, 2, 3), ("WB", 3, 1), ("PROJ", 0),
    ("NORM", 2, 2), ("LN", 2, 3, 0), ("T", 2, 2), ("LN", 2, 3, 1), ("LN", 2, 3, 2), ("LN", 2, 3, 3),
    ("P1", 0), ("PROJ", 1), ("P2", 0), ("F", 2, 2, 0), ("NORM", 2, 3), ("P3", 0), ("P1", 1), ("LN", 3, 1, 0),
    ("T", 2, 3), ("PROJ", 2), ("P2", 1), ("LN", 3, 1, 1), ("VP", 0), ("F", 2, 2, 1), ("P1", 2), ("P3", 1),
    ("LN", 3, 1, 2), ("PROJ", 3), ("LN", 3, 1, 3), ("S", 0, 0), ("P2", 2), ("P1", 3), ("NORM", 3, 1),
    ("F", 2, 3, 1), ("P3", 2), ("P2", 3), ("S", 0, 1), ("F", 2, 3, 0), ("VP", 1), ("S", 1, 0), ("MT", 0),
    ("T", 3, 1), ("P3", 3), ("S", 1, 1),
]

BODY = [
    ("LN", 2, 3, 0, 3), ("WO", -1, 0, 1), ("LN", -1, 4, 0, 2), ("P2", 3, None), ("T", 1, 3, 0),
    ("P3", 3, None), ("PROJ", 4, None), ("MT", 1, None), ("S", 2, 0, None), ("T", -1, 4, 3),
    ("ST", 0, 0, None), ("PV", -1, 1, None), ("VP", 4, 0), ("WO", -1, 1, 1), ("LN", 2, 3, 1, 3),
    ("LN", -1, 4, 1, 2), ("P1", 4, None), ("VP", 4, 2), ("LN", -1, 4, 2, 2), ("LN", 2, 3, 2, 3),
    ("F", -1, 4, 0, 3), ("NRM", -1, None), ("ST", 0, 1, None), ("LN", -1, 4, 3, 2), ("LN", 2, 3, 3, 3),
    ("NORM", -1, 4, 2), ("DT", -1, 0), ("NORM", 2, 3, 3), ("S", 2, 1, None), ("PV", 0, 0, None),
    ("F", -1, 4, 1, 3),
]

TAIL = [
    ("WO", 2, 0), ("WO", 2, 1), ("LN", 4, 2, 0), ("MT", 14), ("ST", 13, 0), ("PV", 12, 1), ("S", 15, 0),
    ("NRM", 12), ("ST", 13, 1), ("PV", 13, 0), ("LN", 4, 2, 1), ("S", 15, 1), ("ST", 14, 0), ("PV", 13, 1),
    ("MT", 15), ("LN", 4, 2, 2), ("ST", 14, 1), ("LN", 4, 2, 3), ("NRM", 13), ("PV", 14, 0), ("NORM", 4, 2),
    ("ST", 15, 0), ("PV", 14, 1), ("T", 4, 2), ("ST", 15, 1), ("NRM", 14), ("PV", 15, 0), ("F", 4, 2, 0),
    ("PV", 15, 1), ("NRM", 15), ("DT", 3), ("WO", 3, 0), ("WO", 3, 1), ("LN", 4, 3, 0), ("LN", 4, 3, 1),
    ("LN", 4, 3, 2), ("LN", 4, 3, 3), ("F", 4, 2, 1), ("NORM", 4, 3), ("KEEP", 1, 24), ("T", 4, 3),
    ("F", 4, 3, 1), ("F", 4, 3, 0),
]
BODY_UNITS = 13


def schedule():
    apart = set(PROLOGUE) | set(TAIL)
    steps = list(PROLOGUE)
    for i in range(BODY_UNITS):
        b, k = divmod(i, KT)
        for kind, where, *rest, when in BODY:
            if when is not None and when != k:
                continue
            if kind == "VP":
                if i + where >= NU:
                    continue
                n, end = (i + where) // 2, NU // 2
            elif when is None:
                n, end = i + where, NU
            else:
                n, end = b + where, B
            st = (kind, rest[0], n, *rest[1:]) if kind in ("T", "LN", "NORM", "F") else (kind, n, *rest)
            if st not in apart and 0 <= n < end:
                steps.append(st)
    return steps + TAIL


JOBS = {"WT": 1, "T": 2, "QKV": 2, "SA": 1, "ET": 1, "OA": 1, "WA": NT, "F": 1, "PROJ": 1, "VP": 1, "MT": 1,
        "PV": 1, "NRM": 1, "DT": 2, "WO": 1, "KEEP": 1}


def xn_slot(s, b):
    return (b % 2, b % 2, 1, 0)[s - 1]


def hybrid_block_kernel(nc, x, Wqkv, bqkv, Wo, bo, wq, wk, wv, wo, qweight, scale, zero, bias, rope, out):
    steps = schedule()
    count, nth = {}, {}
    for st in steps:
        nth[st] = count.get(st[0], 0)
        count[st[0]] = nth[st] + 1
    bank_of, before, owner, turn, scores_on = {}, {}, [None] * BANKS, 0, False
    taken_by_scores = []
    for st in steps:
        if st[0] == "S" and not scores_on:
            scores_on, taken_by_scores = True, [o for o in owner[:6] if o]
        jobs = [(*st, j) for j in range(JOBS.get(st[0], 0))]
        jobs += [("VA", st[1], 0)] if st[0] == "SA" else []
        for job in jobs:
            turn += 1
            bank = 6 + turn % 2 if scores_on else turn % BANKS
            bank_of[job], before[job], owner[bank] = bank, owner[bank], job

    def job_count(job):
        if job[0] == "VA":
            return nth[("SA", job[1])] + 1
        return nth[job[:-1]] * JOBS[job[0]] + job[-1] + 1

    def last_linear(s, b):
        return max((("F", s, b, t, 0) for t in range(NT)), key=job_count)

    xt_slot, xt_before, xn_before, holder, xn_holder = {}, {}, {}, {}, {}
    for st in steps:
        if st[0] == "T":
            s, b = st[1:]
            slot = (b % 2, b % 2, 2, 0)[s - 1]
            xt_slot[st], xt_before[st] = slot, holder.get(slot)
            holder[slot] = {1: ("QKV", b, 1), 2: last_linear(2, b), 3: ("VP", 2 * b + 1, 0), 4: last_linear(4, b)}[s]
        if st[0] == "NORM":
            s, b = st[1:]
            slot = xn_slot(s, b)
            xn_before[st] = xn_holder.get(slot)
            xn_holder[slot] = ("T", s, b, 1)

    def last_reader(job):
        return ("PROJ", job[1] * 2 + 1, 0) if job and job[0] == "VP" else job

    with ExitStack() as ctx:
        def sb(name, shape, dt, where=ctx):
            return where.enter_context(nc.sbuf_tensor(name, shape, dt))

        def sem(name):
            return ctx.enter_context(nc.semaphore(name))

        psum = ctx.enter_context(nc.psum_tensor("psum", [P, BANKS * BANK], F32))

        def bank(k, n=1):
            return psum[:, k * BANK:(k + n) * BANK]

        X = sb("X", [P, B, NT, C], F32)
        wf = sb("wf", [P, KT, C], F32R)
        scale_r = sb("scale_r", [P, C], F32)
        shift_r = sb("shift_r", [P, C], F32)
        row_sum = sb("row_sum", [P, 2, B, NT], F32)
        wb_hi = sb("wb_hi", [P, 4, KT, C], F32R)
        wb_lo = sb("wb_lo", [P, 4, KT, C], F32R)
        XN = sb("XN", [P, 3, NT, C], F32)
        XT_hi = sb("XT_hi", [P, 3, KT, S], F32R)
        XT_lo = sb("XT_lo", [P, 3, KT, S], F32R)
        bias_f = sb("bias_f", [P, C], F32)
        ident = sb("ident", [P, P], F32)
        ident_h = sb("ident_h", [P, P], BF16)
        tri = sb("tri", [P, P], BF16)
        stats = sb("stats", [P, STAT_SLOTS, NT, 6], F32)
        mv = sb("mv", [P, STAT_SLOTS, NT, 2], F32)
        mhalf_var = sb("mhalf_var", [P, STAT_SLOTS, NT], F32)
        rstd = sb("rstd", [P, STAT_SLOTS, NT], F32)
        newton = sb("newton", [P, STAT_SLOTS, NT], F32)
        offset = sb("offset", [P, STAT_SLOTS, NT], F32)

        early = ExitStack()
        stage = sb("stage", [P, 2, KT * C], F32, early)
        q_int = sb("q_int", [P, KT, C // 2], I32, early)
        zero_r = sb("zero_r", [P, C], F32, early)
        wqkv_hi = sb("wqkv_hi", [P, KT, 3 * DA], F32R, early)
        wqkv_lo = sb("wqkv_lo", [P, KT, 3 * DA], F32R, early)
        wo1 = sb("wo1", [P, C], F32, early)
        bias_o = sb("bias_o", [P, C], F32, early)
        bqkv_c = sb("bqkv_c", [P, 3], F32, early)
        qkT = sb("qkT", [P, 2, 2, S], F32, early)
        vT = sb("vT", [P, 2, S], F32, early)
        va = sb("va", [P, 2, NT, DA], F32, early)
        EA = sb("EA", [P, 2, NT, S], F32, early)
        ETs = sb("ETs", [P, 2, NT, S], F32, early)
        OTa = sb("OTa", [P, 2, S], F32, early)
        nmax_a = sb("nmax_a", [P, 2, NT], F32, early)
        sum_a = sb("sum_a", [P, 2, NT], F32, early)
        inv_a = sb("inv_a", [P, 2, NT], F32, early)
        early.close()

        QS = sb("QS", [P, QK_SLOTS, UH, S], BF16)
        KS = sb("KS", [P, QK_SLOTS, UH, S], BF16)
        table = sb("table", [P, 2, S], F32)
        E = sb("E", [P, 2, GH * 3 * P], F32)
        OU = sb("OU", [P, NG, S], F32)
        V = sb("V", [P, V_SLOTS, NT, 2 * UH, 2 * HD], F32)
        parts = sb("parts", [P, 2, 3, 2 * S], BF16)
        SH = sb("SH", [P, 2, 2 * S], F32)
        CC = sb("CC", [P, 2, 2 * S], F32)
        nmax = sb("nmax", [P, 2, NT, UH], F32)
        mrow = sb("mrow", [UH, 2, 2, S], BF16)
        inv_o = sb("inv_o", [P, NG * NT * GH], F32)

        scratch = nc.dram_tensor("qk_parts", (2, 3, 2, P, S), BF16, kind="Internal").ap()

        made = {k: sem(f"made_{k}") for k in [*JOBS, "VA", "S", "ST"]}
        x_loaded = [sem(f"x_loaded{b}") for b in range(B)]
        wqkv_loaded, small_loaded, q_loaded = sem("wqkv_loaded"), sem("small_loaded"), sem("q_loaded")
        wo1_loaded, table_loaded = sem("wo1_loaded"), sem("table_loaded")
        staged = [sem(f"staged{m}") for m in range(4)]
        consts_ready, consts_cleared = sem("consts_ready"), sem("consts_cleared")
        ones_ready = sem("ones_ready")
        wqkv_hi_ready, wqkv_lo_ready = sem("wqkv_hi_ready"), sem("wqkv_lo_ready")
        wf_ready, unpacked, stats_ready, row_shifted = sem("wf_ready"), sem("unpacked"), sem("stats_ready"), sem("row_shifted")
        stat_link, shift_ready = sem("stat_link"), sem("shift_ready")
        wb_hi_ready, wb_lo_ready = sem("wb_hi_ready"), sem("wb_lo_ready")
        xn_ready, bias_added = sem("xn_ready"), sem("bias_added")
        xh_ready, xl_ready = sem("xh_ready"), sem("xl_ready")
        qkv_ready, va_ready, nmax_a_ready = sem("qkv_ready"), sem("va_ready"), sem("nmax_a_ready")
        ea_ready, ea_normed, et_ready, oa_ready = sem("ea_ready"), sem("ea_normed"), sem("et_ready"), sem("oa_ready")
        resid_a, resid_f, resid_o = sem("resid_a"), sem("resid_f"), sem("resid_o")
        rope_parts, roped = sem("rope_parts"), sem("roped")
        part1_ready, rest1_ready, part2_ready, part3_ready = sem("part1"), sem("rest1"), sem("part2"), sem("part3")
        v_ready, max_ready, m1_ready, m2_ready = sem("v_ready"), sem("max_ready"), sem("m1_ready"), sem("m2_ready")
        exp_ready, masked, ou_ready, o_ready = sem("exp_ready"), sem("masked"), sem("ou_ready"), sem("o_ready")
        oh_ready, ol_ready = sem("oh_ready"), sem("ol_ready")
        parts_stored = [sem(f"parts_stored{i}") for i in range(2)]
        qk_loaded = [sem(f"qk_loaded{i}") for i in range(QK_SLOTS)]
        m_loaded = [sem(f"m_loaded{i}") for i in range(2)]
        out_done = sem("out_done")
        dve_link, pool_link = sem("dve_link"), sem("pool_link")

        released = {"WT": wf_ready, "T": xl_ready, "QKV": qkv_ready, "VA": va_ready, "SA": ea_ready,
                    "ET": et_ready, "OA": oa_ready, "WA": resid_a, "F": resid_f, "PROJ": rope_parts,
                    "VP": v_ready, "MT": m2_ready, "PV": ou_ready, "NRM": o_ready, "DT": ol_ready,
                    "WO": resid_o, "KEEP": made["KEEP"]}

        def wait_job(eng, job):
            eng.wait_ge(made[job[0]], job_count(job))

        def projections_over(eng):
            eng.wait_ge(made["QKV"], 2 * B)

        def staging_over(eng):
            projections_over(eng)
            eng.wait_ge(wb_lo_ready, 2 * 4)
            eng.wait_ge(wf_ready, KT)
            eng.wait_ge(shift_ready, 1)

        def attention_over(eng):
            eng.wait_ge(resid_a, B * NT)

        bqkv_v = bqkv.rearrange("(j p) -> p j", p=P)
        x_v = x.rearrange("b (t p) n -> b p t n", p=P)
        out_v = out.rearrange("b (t p) n -> b p t n", p=P)

        def rows(w):
            return w.rearrange("(k p) n -> p k n", p=P)

        def staging(m):
            return stage[:, m % 2, :].rearrange("p (k n) -> p k n", k=KT)

        block = ctx.enter_context(nc.Block())

        @block.sync
        def _(sp):
            sp.dma_start(X[:, 0], x_v[0]).then_inc(x_loaded[0], 16)
            sp.dma_start(stage[:, 0, 0:KT * 3 * DA].rearrange("p (k n) -> p k n", k=KT),
                         rows(Wqkv)).then_inc(wqkv_loaded, 16)
            sp.dma_start(X[:, 1], x_v[1]).then_inc(x_loaded[1], 16)
            sp.dma_start(bqkv_c[:], bqkv_v, allow_slow_non_contiguous=True).then_inc(small_loaded, 16)
            sp.dma_start(scale_r[:], scale.rearrange("n a -> (n a)").partition_broadcast(P)).then_inc(small_loaded, 16)
            sp.dma_start(zero_r[:], zero.rearrange("n a -> (n a)").partition_broadcast(P)).then_inc(small_loaded, 16)
            sp.dma_start(bias_o[:], bo.partition_broadcast(P)).then_inc(small_loaded, 16)
            sp.dma_start(bias_f[:], bias.partition_broadcast(P)).then_inc(small_loaded, 16)
            sp.dma_start(q_int[:], rows(qweight)).then_inc(q_loaded, 16)
            sp.dma_start(wo1[:], Wo).then_inc(wo1_loaded, 16)
            sp.dma_start(X[:, 2], x_v[2]).then_inc(x_loaded[2], 16)
            sp.dma_start(X[:, 3], x_v[3]).then_inc(x_loaded[3], 16)
            for m, w in enumerate((wq, wk, wv, wo)):
                if m == 0:
                    sp.wait_ge(unpacked, 1)
                elif m == 1:
                    sp.wait_ge(made["WT"], KT)
                else:
                    sp.wait_ge(wb_lo_ready, 2 * (m - 1))
                sp.dma_start(staging(m), rows(w)).then_inc(staged[m], 16)
            projections_over(sp)
            sp.dma_start(table[:], rope).then_inc(table_loaded, 16)
            for st in steps:
                if st[0] == "P3":
                    u = st[1]
                    sp.wait_ge(part3_ready, u + 1)
                    if u >= 2:
                        sp.wait_ge(qk_loaded[(u - 2) % QK_SLOTS], 16 * 2 * len(Q_PARTS) * ((u - 2) // QK_SLOTS + 1))
                    sp.dma_start(scratch[u % 2].rearrange("c a d t -> d (c a) t"),
                                 parts[:, u % 2].rearrange("p c (a t) -> p (c a) t", a=2)
                                 ).then_inc(parts_stored[u % 2], 16)
                    sp.wait_ge(parts_stored[u % 2], 16 * (u // 2 + 1))
                    if u == 0:
                        staging_over(sp)
                    if u >= QK_SLOTS:
                        sp.wait_ge(made["ST"], nth[("ST", u - QK_SLOTS, NG - 1)] + 1)
                    for a, (stack, which) in enumerate(((QS, Q_PARTS), (KS, K_PARTS))):
                        for row, c in enumerate(which):
                            sp.dma_start(stack[row * HD:(row + 1) * HD, u % QK_SLOTS],
                                         scratch[u % 2, c, a].rearrange("(h d) t -> d h t", d=HD)
                                         ).then_inc(qk_loaded[u % QK_SLOTS], 16)
                if st[0] == "MT":
                    u = st[1]
                    sp.wait_ge(m2_ready, nth[st] + 1)
                    sp.wait_ge(m1_ready, nth[st] + 1)
                    for r in range(2):
                        sp.dma_start(QS[KROWS + r:KROWS + r + 1, u % QK_SLOTS], mrow[:, u % 2, r]
                                     ).then_inc(m_loaded[u % 2], 16)
                if st[0] == "F" and st[1] == 4:
                    b, t = st[2:]
                    sp.wait_ge(resid_f, nth[st] + 1)
                    sp.dma_start(out_v[b][:, t], X[:, b, t]).then_inc(out_done, 16)
            sp.wait_ge(out_done, 16 * B * NT)

        @block.gpsimd
        def _(pool):
            links = [0]

            def link(ins):
                links[0] += 1
                ins.then_inc(pool_link, 1)
                pool.wait_ge(pool_link, links[0])

            nc.gpsimd.memset(ident[:], 0.0).then_inc(consts_cleared, 1)
            nc.gpsimd.memset(ident_h[:], 0.0).then_inc(consts_cleared, 1)
            nc.gpsimd.memset(tri[:], 0.0).then_inc(consts_cleared, 1)
            pool.wait_ge(consts_cleared, 3)
            for m in (ident, ident_h):
                nc.gpsimd.affine_select(out=m[:], in_=m[:], compare_op=ALU.not_equal, fill=1.0, base=0,
                                        pattern=[[-1, P]], channel_multiplier=1).then_inc(consts_ready, 1)
            nc.gpsimd.affine_select(out=tri[:], in_=tri[:], compare_op=ALU.is_ge, fill=MASKED, base=0,
                                    pattern=[[-1, P]], channel_multiplier=1).then_inc(consts_ready, 1)
            met = dict.fromkeys(("NORM", "WB", "PROJ", "P1"), 0)
            for st in steps:
                if st[0] in met and st[:2] != ("NORM", 3):
                    met[st[0]] += 1
                if st[0] == "NORM" and st[1] != 3:
                    s, b = st[1:]
                    pool.wait_ge(xn_ready, nth[st] + 1)
                    if s == 1 and b == 0:
                        pool.wait_ge(small_loaded, 16 * 5)
                    for t in range(NT):
                        nc.gpsimd.tensor_tensor(X[:, b, t], X[:, b, t], (bias_o if s == 1 else bias_f)[:], ALU.add
                                                ).then_inc(bias_added, 1)
                if st[0] == "WQ":
                    pool.wait_ge(wqkv_loaded, 16)
                    pool.wait_ge(wqkv_hi_ready, 1)
                    nc.gpsimd.tensor_tensor(wqkv_lo[:].rearrange("p k n -> p (k n)"), stage[:, 0, 0:KT * 3 * DA],
                                            wqkv_hi[:].bitcast(F32).rearrange("p k n -> p (k n)"), ALU.subtract
                                            ).then_inc(wqkv_lo_ready, 1)
                if st[0] == "WB":
                    m, part = st[1], slice(2 * st[2], 2 * st[2] + 2)
                    pool.wait_ge(staged[m], 16)
                    pool.wait_ge(wb_hi_ready, nth[st] + 1)
                    nc.gpsimd.tensor_tensor(wb_lo[:, m, part], staging(m)[:, part], wb_hi[:, m, part].bitcast(F32),
                                            ALU.subtract).then_inc(wb_lo_ready, 1)
                if st[0] == "PROJ":
                    u = st[1]
                    if u == 0:
                        pool.wait_ge(table_loaded, 16)
                    pool.wait_ge(rope_parts, u + 1)
                    sh = SH[:, u % 2].rearrange("p (a t) -> p a t", a=2)
                    link(nc.gpsimd.tensor_tensor(sh, sh, table[:, 1:2, :].to_broadcast((P, 2, S)), ALU.mult))
                    nc.gpsimd.tensor_tensor(SH[:, u % 2], SH[:, u % 2], CC[:, u % 2], ALU.add).then_inc(roped, 1)
                if st[0] == "VP" and st[1] == 0:
                    staging_over(pool)
                    attention_over(pool)
                    pool.wait_ge(bias_added, met["NORM"] * NT)
                    pool.wait_ge(wb_lo_ready, met["WB"])
                    if met["PROJ"]:
                        pool.wait_ge(roped, met["PROJ"])
                    if met["P1"]:
                        pool.wait_ge(rest1_ready, met["P1"])
                    nc.gpsimd.memset(KS[KROWS:P].bitcast(F32), TWO_ONES).then_inc(ones_ready, 1)
                    pool.wait_ge(ones_ready, 1)
                    nc.gpsimd.memset(V[:, :, :, :, HD:], 1.0).then_inc(ones_ready, 1)
                if st[0] == "P1":
                    u = st[1]
                    pool.wait_ge(roped, u + 1)
                    pool.wait_ge(part1_ready, u + 1)
                    nc.gpsimd.tensor_tensor(SH[:, u % 2], SH[:, u % 2], parts[:, u % 2, 0], ALU.subtract
                                            ).then_inc(rest1_ready, 1)
                if st[0] == "ST":
                    n = nth[st]
                    pool.wait_ge(exp_ready, n + 1)
                    for at, width in ((0, S), (GH * S, P)):
                        e = E[:, n % 2, at:at + GH * width].rearrange("p (h q) -> p h q", h=GH)[:, :, 0:P]
                        last = nc.gpsimd.affine_select(out=e, in_=e, compare_op=ALU.is_ge, fill=0.0, base=0,
                                                       pattern=[[0, GH], [1, P]], channel_multiplier=-1)
                    last.then_inc(masked, 1)

        @block.scalar
        def _(act):
            def copy(out_, in_):
                return nc.scalar.activation(out_, in_, ACT.Copy)

            for st in steps:
                k = st[0]
                if k == "WQ":
                    act.wait_ge(wqkv_loaded, 16)
                    copy(wqkv_hi[:].rearrange("p k n -> p (k n)"), stage[:, 0, 0:KT * 3 * DA]
                         ).then_inc(wqkv_hi_ready, 1)
                elif k == "WB":
                    m, part = st[1], slice(2 * st[2], 2 * st[2] + 2)
                    act.wait_ge(staged[m], 16)
                    copy(wb_hi[:, m, part], staging(m)[:, part]).then_inc(wb_hi_ready, 1)
                elif k == "WT":
                    wait_job(act, (*st, 0))
                    copy(wf[:, st[1]], bank(bank_of[(*st, 0)])).then_inc(wf_ready, 1)
                elif k == "NORM":
                    s, b = st[1:]
                    sl = nth[st] % STAT_SLOTS
                    act.wait_ge(stats_ready, nth[st] + 1)
                    if xn_before[st]:
                        wait_job(act, xn_before[st])
                    for t in range(NT):
                        more = {"accum_out": row_sum[:, s // 2 - 1, b, t:t + 1]} if s in (2, 4) else {}
                        last = nc.scalar.activation(XN[:, xn_slot(s, b), t], X[:, b, t], ACT.Identity,
                                                    bias=offset[:, sl, t:t + 1], scale=rstd[:, sl, t:t + 1], **more)
                    last.then_inc(xn_ready, 1)
                elif k == "T":
                    slot = xt_slot[st]
                    for j in range(2):
                        wait_job(act, (*st, j))
                        if j == 0 and xt_before[st]:
                            wait_job(act, last_reader(xt_before[st]))
                        copy(XT_hi[:, slot, 2 * j:2 * j + 2].rearrange("p k n -> p (k n)"),
                             bank(bank_of[(*st, j)])).then_inc(xh_ready, 1)
                elif k == "QKV":
                    b = st[1]
                    wait_job(act, (*st, 0))
                    if b == 0:
                        act.wait_ge(small_loaded, 16 * 5)
                    if b >= 2:
                        wait_job(act, ("SA", b - 2, 0))
                    ps = bank(bank_of[(*st, 0)])
                    nc.scalar.activation(qkT[:, b % 2, 0], ps[:, 0:S], ACT.Identity, bias=bqkv_c[:, 0:1])
                    nc.scalar.activation(qkT[:, b % 2, 1], ps[:, S:2 * S], ACT.Identity, bias=bqkv_c[:, 1:2]
                                         ).then_inc(qkv_ready, 1)
                    wait_job(act, (*st, 1))
                    if b >= 2:
                        wait_job(act, ("VA", b - 2, 0))
                    nc.scalar.activation(vT[:, b % 2], bank(bank_of[(*st, 1)])[:, 0:S], ACT.Identity,
                                         bias=bqkv_c[:, 2:3]).then_inc(qkv_ready, 1)
                elif k == "SA":
                    b = st[1]
                    wait_job(act, ("VA", b, 0))
                    if b >= 2:
                        wait_job(act, ("OA", b - 2, 0))
                    copy(va[:, b % 2].rearrange("p t d -> p (t d)"), bank(bank_of[("VA", b, 0)])[:, 0:NT * DA]
                         ).then_inc(va_ready, 1)
                elif k == "SM":
                    b = st[1]
                    act.wait_ge(nmax_a_ready, b + 1)
                    if b >= 2:
                        wait_job(act, ("ET", b - 2, 0))
                    ps = bank(bank_of[("SA", b, 0)])
                    for t in range(NT):
                        last = nc.scalar.activation(EA[:, b % 2, t], ps[:, t * S:(t + 1) * S], ACT.Exp,
                                                    bias=nmax_a[:, b % 2, t:t + 1], scale=float(DA) ** -0.5,
                                                    accum_out=sum_a[:, b % 2, t:t + 1])
                    last.then_inc(ea_ready, 1)
                elif k == "ET":
                    b = st[1]
                    wait_job(act, (*st, 0))
                    if b >= 2:
                        wait_job(act, ("OA", b - 2, 0))
                    copy(ETs[:, b % 2].rearrange("p k q -> p (k q)"), bank(bank_of[(*st, 0)])).then_inc(et_ready, 1)
                elif k == "OA":
                    b = st[1]
                    wait_job(act, (*st, 0))
                    if b >= 2:
                        wait_job(act, ("WA", b - 2, NT - 1))
                    copy(OTa[:, b % 2], bank(bank_of[(*st, 0)])[:, 0:S]).then_inc(oa_ready, 1)
                elif k == "P1":
                    u = st[1]
                    act.wait_ge(roped, u + 1)
                    if u >= 2:
                        act.wait_ge(parts_stored[u % 2], 16 * (u // 2))
                    copy(parts[:, u % 2, 0], SH[:, u % 2]).then_inc(part1_ready, 1)
                elif k == "P2":
                    u = st[1]
                    act.wait_ge(rest1_ready, u + 1)
                    copy(parts[:, u % 2, 1], SH[:, u % 2]).then_inc(part2_ready, 1)
                elif k == "VP":
                    v = st[1]
                    wait_job(act, (*st, 0))
                    if v == 0:
                        act.wait_ge(ones_ready, 2)
                    if v >= V_SLOTS:
                        wait_job(act, ("PV", 2 * (v - V_SLOTS) + 1, NG - 1, 0))
                    copy(V[:, v % V_SLOTS, :, :, 0:HD],
                         bank(bank_of[(*st, 0)]).rearrange("p (t h d) -> p t h d", t=NT, d=HD)).then_inc(v_ready, 1)
                elif k == "MT":
                    u = st[1]
                    wait_job(act, (*st, 0))
                    if u >= 2:
                        act.wait_ge(m_loaded[u % 2], 32 * (u // 2))
                    copy(mrow[:, u % 2, 0], bank(bank_of[(*st, 0)])[0:UH, 0:S]).then_inc(m1_ready, 1)
                elif k == "ST":
                    n = nth[st]
                    if n == 0:
                        attention_over(act)
                    act.wait_ge(made["ST"], n + 1)
                    if n >= 2:
                        wait_job(act, ("PV", *divmod(n - 2, NG), 0))
                    nc.scalar.activation(E[:, n % 2], bank(3, 3), ACT.Exp, scale=float(HD) ** -0.5
                                         ).then_inc(exp_ready, 1)
                elif k == "PV":
                    u, g = st[1:]
                    wait_job(act, (*st, 0))
                    if u:
                        wait_job(act, ("NRM", u - 1, 0))
                    copy(OU[:, g], bank(bank_of[(*st, 0)])[:, 0:S]).then_inc(ou_ready, 1)
                elif k == "DT":
                    b = st[1]
                    for j in range(2):
                        wait_job(act, (*st, j))
                        if j == 0:
                            wait_job(act, ("WO", b - 1, NT - 1, 0) if b else last_linear(2, B - 1))
                        copy(XT_hi[:, 1, 2 * j:2 * j + 2].rearrange("p k n -> p (k n)"), bank(bank_of[(*st, j)])
                             ).then_inc(oh_ready, 1)

        @block.vector
        def _(dve):
            links = [0]
            bias_n = {}
            stat_links = {"made": 0}
            for st in steps:
                if st[0] == "NORM" and st[1] != 3:
                    bias_n[st[1:]] = (len(bias_n) + 1) * NT

            def link(ins):
                links[0] += 1
                ins.then_inc(dve_link, 1)
                dve.wait_ge(dve_link, links[0])

            def add_residual(job, b, t, sem_):
                wait_job(dve, job)
                nc.vector.tensor_tensor(X[:, b, t], X[:, b, t], bank(bank_of[job]), ALU.add).then_inc(sem_, 1)

            for st in steps:
                k = st[0]
                if k == "DQ":
                    dve.wait_ge(q_loaded, 16)
                    dve.wait_ge(wqkv_lo_ready, 1)
                    w_int = stage[:, 0, :].bitcast(I32).rearrange("p (k n) -> p k n", k=KT)
                    w = stage[:, 0, :].bitcast(I32).rearrange("p (j i e) -> p j i e", j=KT, e=2)
                    nc.vector.tensor_scalar(w[:, :, :, 0], q_int[:], 4, 15, ALU.logical_shift_right, ALU.bitwise_and)
                    link(nc.vector.tensor_scalar(w[:, :, :, 1], q_int[:], 15, None, ALU.bitwise_and))
                    nc.vector.tensor_copy(staging(1), w_int).then_inc(unpacked, 1)
                    dve.wait_ge(small_loaded, 16 * 5)
                    nc.vector.scalar_tensor_tensor(shift_r[:], zero_r[:], -1.0, scale_r[:], ALU.mult, ALU.mult
                                                   ).then_inc(shift_ready, 1)
                    dve.wait_ge(shift_ready, 1)
                elif k == "LN":
                    sn, b, q = st[1:]
                    n = nth[("NORM", sn, b)]
                    sl = n % STAT_SLOTS
                    y, v, w = rstd[:, sl], mhalf_var[:, sl], newton[:, sl]
                    for p in STAT_PARTS[q]:
                        if p == 0:
                            if sn == 1:
                                dve.wait_ge(x_loaded[b], 16)
                            elif sn == 2:
                                dve.wait_ge(resid_a, (b + 1) * NT)
                            elif sn == 3:
                                dve.wait_ge(resid_f, job_count(last_linear(2, b)))
                            else:
                                dve.wait_ge(resid_o, (b + 1) * NT)
                            if n >= STAT_SLOTS:
                                dve.wait_ge(xn_ready, n - STAT_SLOTS + 1)
                            for t in range(NT):
                                last = nc.vector.bn_stats(stats[:, sl, t], X[:, b, t])
                        else:
                            dve.wait_ge(stat_link, stat_links[(sn, b)])
                        if p == 1:
                            for t in range(NT):
                                last = nc.vector.bn_aggr(mv[:, sl, t], stats[:, sl, t])
                        elif p == 2:
                            last = nc.vector.tensor_scalar(v, mv[:, sl, :, 1], EPS, -0.5, ALU.add, ALU.mult)
                        elif p == 3:
                            last = nc.vector.tensor_scalar(y.bitcast(I32), v.bitcast(I32), -0.5, RSQRT_MAGIC,
                                                           ALU.mult, ALU.add)
                        elif p == STAT_LINKS - 1:
                            last = nc.vector.scalar_tensor_tensor(offset[:, sl], mv[:, sl, :, 0], -1.0, y,
                                                                  ALU.mult, ALU.mult)
                        elif p >= 4 and p % 2 == 0:
                            for t in range(NT):
                                last = nc.vector.scalar_tensor_tensor(w[:, t:t + 1], y[:, t:t + 1], v[:, t:t + 1],
                                                                      y[:, t:t + 1], ALU.mult, ALU.mult)
                        elif p >= 4:
                            last = nc.vector.scalar_tensor_tensor(y, w, 1.5, y, ALU.add, ALU.mult)
                        if p == STAT_LINKS - 1:
                            last.then_inc(stats_ready, 1)
                        else:
                            stat_links[(sn, b)] = stat_links["made"] = stat_links["made"] + 1
                            last.then_inc(stat_link, 1)
                elif k == "T":
                    slot = xt_slot[st]
                    for j in range(2):
                        dve.wait_ge(xh_ready, nth[st] * 2 + j + 1)
                        if j == 0 and xt_before[st]:
                            wait_job(dve, last_reader(xt_before[st]))
                        nc.vector.tensor_tensor(XT_lo[:, slot, 2 * j:2 * j + 2].rearrange("p k n -> p (k n)"),
                                                bank(bank_of[(*st, j)]),
                                                XT_hi[:, slot, 2 * j:2 * j + 2].bitcast(F32).rearrange("p k n -> p (k n)"),
                                                ALU.subtract).then_inc(xl_ready, 1)
                elif k == "SA":
                    b = st[1]
                    wait_job(dve, (*st, 0))
                    if b >= 2:
                        dve.wait_ge(ea_ready, b - 1)
                    link(nc.vector.tensor_reduce(nmax_a[:, b % 2], bank(bank_of[(*st, 0)]).rearrange(
                        "p (t k) -> p t k", t=NT), AX, ALU.max))
                    nc.vector.tensor_scalar(nmax_a[:, b % 2], nmax_a[:, b % 2], -float(DA) ** -0.5, None, ALU.mult
                                            ).then_inc(nmax_a_ready, 1)
                elif k == "SM":
                    b = st[1]
                    dve.wait_ge(ea_ready, b + 1)
                    link(nc.vector.reciprocal(inv_a[:, b % 2], sum_a[:, b % 2]))
                    for t in range(NT):
                        last = nc.vector.tensor_scalar(EA[:, b % 2, t], EA[:, b % 2, t], inv_a[:, b % 2, t:t + 1], None,
                                                       ALU.mult)
                    last.then_inc(ea_normed, 1)
                elif k == "WA":
                    b = st[1]
                    dve.wait_ge(bias_added, bias_n[(1, b)])
                    for t in range(NT):
                        add_residual((*st, t), b, t, resid_a)
                elif k == "F":
                    sn, b, t = st[1:]
                    dve.wait_ge(bias_added, bias_n[(sn, b)])
                    nc.vector.scalar_tensor_tensor(X[:, b, t], shift_r[:], row_sum[:, sn // 2 - 1, b, t:t + 1],
                                                   X[:, b, t], ALU.mult, ALU.add).then_inc(row_shifted, 1)
                    wait_job(dve, (*st, 0))
                    prod = bank(bank_of[(*st, 0)])
                    link(nc.vector.tensor_tensor(prod, prod, scale_r[:], ALU.mult))
                    dve.wait_ge(row_shifted, nth[st] + 1)
                    nc.vector.tensor_tensor(X[:, b, t], X[:, b, t], prod, ALU.add).then_inc(resid_f, 1)
                elif k == "DT":
                    b = st[1]
                    for j in range(2):
                        dve.wait_ge(oh_ready, b * 2 + j + 1)
                        if j == 0:
                            wait_job(dve, ("WO", b - 1, NT - 1, 0) if b else last_linear(2, B - 1))
                        nc.vector.tensor_tensor(XT_lo[:, 1, 2 * j:2 * j + 2].rearrange("p k n -> p (k n)"),
                                                bank(bank_of[(*st, j)]),
                                                XT_hi[:, 1, 2 * j:2 * j + 2].bitcast(F32).rearrange("p k n -> p (k n)"),
                                                ALU.subtract).then_inc(ol_ready, 1)
                elif k == "WO":
                    add_residual((*st, 0), st[1], st[2], resid_o)
                elif k == "PROJ":
                    u = st[1]
                    if u == 0:
                        dve.wait_ge(table_loaded, 16)
                    wait_job(dve, (*st, 0))
                    if u >= 2:
                        dve.wait_ge(part3_ready, u - 1)
                        dve.wait_ge(roped, u - 1)
                    ps = bank(bank_of[(*st, 0)])
                    nc.vector.stream_shuffle(SH[:, u % 2], ps, [i ^ 1 for i in range(32)])
                    nc.vector.tensor_tensor(CC[:, u % 2].rearrange("p (a t) -> p a t", a=2),
                                            ps.rearrange("p (a t) -> p a t", a=2),
                                            table[:, 0:1, :].to_broadcast((P, 2, S)), ALU.mult
                                            ).then_inc(rope_parts, 1)
                elif k == "P3":
                    u = st[1]
                    dve.wait_ge(part2_ready, u + 1)
                    nc.vector.tensor_tensor(parts[:, u % 2, 2], SH[:, u % 2], parts[:, u % 2, 1], ALU.subtract
                                            ).then_inc(part3_ready, 1)
                elif k == "S":
                    u, g = st[1:]
                    dve.wait_ge(made["S"], nth[st] + 1)
                    if g == 0 and u >= 2:
                        wait_job(dve, ("MT", u - 2, 0))
                    nc.vector.tensor_reduce(nmax[:, u % 2, 0, g * GH:(g + 1) * GH],
                                            bank(0).rearrange("p (h k) -> p h k", h=GH), AX, ALU.max, negate=True)
                    nc.vector.tensor_reduce(nmax[:, u % 2, 1, g * GH:(g + 1) * GH],
                                            bank(1, 2).rearrange("p (h k) -> p h k", h=GH), AX, ALU.max, negate=True
                                            ).then_inc(max_ready, 1)
                elif k == "MT":
                    u = st[1]
                    dve.wait_ge(m1_ready, nth[st] + 1)
                    nc.vector.tensor_tensor(mrow[:, u % 2, 1], bank(bank_of[(*st, 0)])[0:UH, 0:S], mrow[:, u % 2, 0],
                                            ALU.subtract).then_inc(m2_ready, 1)
                elif k == "NRM":
                    u = st[1]
                    b, m = divmod(u, KT)
                    wait_job(dve, (*st, 0))
                    ps = bank(bank_of[(*st, 0)]).rearrange("p (g t h d) -> p g t h d", g=NG, t=NT, h=GH)
                    inv = inv_o[:].rearrange("p (g t h) -> p g t h", g=NG, t=NT)
                    link(nc.vector.reciprocal(inv, ps[:, :, :, :, HD]))
                    if m == 0 and b:
                        wait_job(dve, ("DT", b - 1, 1))
                    for t in range(NT):
                        o = XN[:, 2, t, m * P:(m + 1) * P].rearrange("p (g h d) -> p g h d", g=NG, h=GH)
                        last = nc.vector.tensor_tensor(
                            o, ps[:, :, t, :, 0:HD],
                            inv[:, :, t, :].unsqueeze(3).to_broadcast((P, NG, GH, HD)), ALU.mult)
                    last.then_inc(o_ready, 1)

        @block.tensor
        def _(pe):
            def take(job):
                if before[job]:
                    pe.wait_ge(released[before[job][0]], job_count(before[job]))
                return bank(bank_of[job])

            def three_pass(out_, stat, mov, first, last):
                nc.tensor.matmul(out_, stat[0], mov[1], start=first, stop=False)
                nc.tensor.matmul(out_, stat[1], mov[0], start=False, stop=False)
                return nc.tensor.matmul(out_, stat[0], mov[0], start=False, stop=last)

            scores_on = False
            for st in steps:
                k = st[0]
                if k == "WT":
                    if st[1] == 0:
                        pe.wait_ge(unpacked, 1)
                        pe.wait_ge(consts_ready, 3)
                    ps = take((*st, 0))
                    for j in range(KT):
                        last = nc.tensor.transpose(ps[:, j * P:(j + 1) * P],
                                                   staging(1)[:, j, st[1] * P:(st[1] + 1) * P], ident[:])
                    last.then_inc(made[k], 1)
                elif k == "KEEP":
                    if nth[st] == 0:
                        pe.wait_ge(consts_ready, 3)
                    ps = take((*st, 0))
                    for _ in range(st[2]):
                        last = nc.tensor.matmul(ps.rearrange("p (j n) -> p j n", n=P), ident_h[:],
                                                ident_h[:].unsqueeze(1).to_broadcast((P, BANK // P, P)),
                                                start=True, stop=True)
                    last.then_inc(made[k], 1)
                elif k == "T":
                    s, b = st[1:]
                    slot = xn_slot(s, b)
                    if nth[st] == 0:
                        pe.wait_ge(consts_ready, 3)
                    pe.wait_ge(xn_ready, nth[("NORM", s, b)] + 1)
                    for j in range(2):
                        ps = take((*st, j))
                        for kk in range(2):
                            for t in range(NT):
                                c = (2 * j + kk) * P
                                last = nc.tensor.transpose(ps[:, kk * S + t * P:kk * S + (t + 1) * P],
                                                           XN[:, slot, t, c:c + P], ident[:])
                        last.then_inc(made[k], 1)
                elif k == "QKV":
                    b = st[1]
                    pe.wait_ge(xl_ready, (nth[("T", 1, b)] + 1) * 2)
                    pe.wait_ge(xh_ready, (nth[("T", 1, b)] + 1) * 2)
                    pe.wait_ge(wqkv_lo_ready, 1)
                    for j, blocks in enumerate(((0, 1), (2,))):
                        ps = take((*st, j))
                        for i, m in enumerate(blocks):
                            for kt in range(KT):
                                last = three_pass(ps[:, i * S:(i + 1) * S],
                                                  [w[:, kt, m * DA:(m + 1) * DA] for w in (wqkv_hi, wqkv_lo)],
                                                  [xt[:, b % 2, kt] for xt in (XT_hi, XT_lo)],
                                                  kt == 0, kt == KT - 1)
                        last.then_inc(made[k], 1)
                elif k == "SA":
                    b = st[1]
                    pe.wait_ge(qkv_ready, 2 * (b + 1))
                    ps = take((*st, 0))
                    for t in range(NT):
                        last = nc.tensor.matmul(ps[:, t * S:(t + 1) * S], qkT[:, b % 2, 0, t * P:(t + 1) * P],
                                                qkT[:, b % 2, 1], start=True, stop=True)
                    last.then_inc(made[k], 1)
                    ps = take(("VA", b, 0))
                    for t in range(NT):
                        last = nc.tensor.transpose(ps[:, t * DA:(t + 1) * DA], vT[:, b % 2, t * P:(t + 1) * P], ident[:])
                    last.then_inc(made["VA"], 1)
                elif k == "ET":
                    b = st[1]
                    pe.wait_ge(ea_normed, b + 1)
                    ps = take((*st, 0))
                    for kt in range(NT):
                        for t in range(NT):
                            last = nc.tensor.transpose(ps[:, kt * S + t * P:kt * S + (t + 1) * P],
                                                       EA[:, b % 2, t, kt * P:(kt + 1) * P], ident[:])
                    last.then_inc(made[k], 1)
                elif k == "OA":
                    b = st[1]
                    pe.wait_ge(et_ready, b + 1)
                    pe.wait_ge(va_ready, b + 1)
                    ps = take((*st, 0))
                    for kt in range(NT):
                        last = nc.tensor.matmul(ps[:, 0:S], va[:, b % 2, kt], ETs[:, b % 2, kt],
                                                start=kt == 0, stop=kt == NT - 1)
                    last.then_inc(made[k], 1)
                elif k == "WA":
                    b = st[1]
                    pe.wait_ge(oa_ready, b + 1)
                    if b == 0:
                        pe.wait_ge(wo1_loaded, 16)
                    for t in range(NT):
                        ps = take((*st, t))
                        nc.tensor.matmul(ps, OTa[:, b % 2, t * P:(t + 1) * P], wo1[:], start=True, stop=True
                                         ).then_inc(made[k], 1)
                elif k == "F":
                    s, b, t = st[1:]
                    tn = nth[("T", s, b)]
                    slot = xt_slot[("T", s, b)]
                    pe.wait_ge(xl_ready, (tn + 1) * 2)
                    pe.wait_ge(xh_ready, (tn + 1) * 2)
                    pe.wait_ge(wf_ready, KT)
                    ps = take((*st, 0))
                    for kt in range(KT):
                        tok = slice(t * P, (t + 1) * P)
                        nc.tensor.matmul(ps, XT_lo[:, slot, kt, tok], wf[:, kt], start=kt == 0, stop=False)
                        last = nc.tensor.matmul(ps, XT_hi[:, slot, kt, tok], wf[:, kt], start=False,
                                                stop=kt == KT - 1)
                    last.then_inc(made[k], 1)
                elif k == "PROJ":
                    u = st[1]
                    b, m = divmod(u, KT)
                    pe.wait_ge(xl_ready, (nth[("T", 3, b)] + 1) * 2)
                    pe.wait_ge(xh_ready, (nth[("T", 3, b)] + 1) * 2)
                    if u == 0:
                        pe.wait_ge(wb_hi_ready, 2 * 2)
                        pe.wait_ge(wb_lo_ready, 2 * 2)
                    ps = take((*st, 0))
                    for a in range(2):
                        for kt in range(KT):
                            last = three_pass(ps[:, a * S:(a + 1) * S],
                                              [w[:, a, kt, m * P:(m + 1) * P] for w in (wb_hi, wb_lo)],
                                              [xt[:, 2, kt] for xt in (XT_hi, XT_lo)], kt == 0, kt == KT - 1)
                    last.then_inc(made[k], 1)
                elif k == "VP":
                    m = st[1] % 2
                    pe.wait_ge(xl_ready, (nth[("T", 3, st[1] // 2)] + 1) * 2)
                    pe.wait_ge(xh_ready, (nth[("T", 3, st[1] // 2)] + 1) * 2)
                    if st[1] == 0:
                        pe.wait_ge(wb_hi_ready, 2 * 3)
                        pe.wait_ge(wb_lo_ready, 2 * 3)
                    ps = take((*st, 0))
                    for t in range(NT):
                        for kt in range(KT):
                            last = three_pass(ps[:, t * S:(t + 1) * S],
                                              [xt[:, 2, kt, t * P:(t + 1) * P] for xt in (XT_hi, XT_lo)],
                                              [w[:, 2, kt, m * S:(m + 1) * S] for w in (wb_hi, wb_lo)],
                                              kt == 0, kt == KT - 1)
                    last.then_inc(made[k], 1)
                elif k == "S":
                    u, g = st[1:]
                    slot = u % QK_SLOTS
                    pe.wait_ge(qk_loaded[slot], 16 * 2 * len(Q_PARTS) * (u // QK_SLOTS + 1))
                    if not scores_on:
                        scores_on = True
                        for job in taken_by_scores:
                            pe.wait_ge(released[job[0]], job_count(job))
                    if nth[st]:
                        pe.wait_ge(max_ready, nth[st])
                    nc.tensor.matmul(bank(0).rearrange("p (h k) -> p h k", h=GH), ident_h[:],
                                     tri[:].unsqueeze(1).to_broadcast((P, GH, P)),
                                     start=True, stop=False, skip_group_check=True)
                    for half in range(2):
                        nc.tensor.matmul(bank(1 + half).rearrange("p (h k) -> p h k", h=2)[:, :, P:S], ident_h[:],
                                         tri[:].unsqueeze(1).to_broadcast((P, 2, P)),
                                         start=True, stop=False, skip_group_check=True)
                    for j in range(GH):
                        h = g * GH + j
                        nc.tensor.matmul(bank(0)[:, j * P:(j + 1) * P], QS[0:KROWS, slot, h, 0:P],
                                         KS[0:KROWS, slot, h, 0:P], start=False, stop=True, skip_group_check=True)
                        last = nc.tensor.matmul(bank(1, 2)[:, j * S:(j + 1) * S], QS[0:KROWS, slot, h, P:S],
                                                KS[0:KROWS, slot, h, :], start=False, stop=True, skip_group_check=True)
                    last.then_inc(made[k], 1)
                elif k == "MT":
                    u = st[1]
                    pe.wait_ge(max_ready, nth[("S", u, NG - 1)] + 1)
                    ps = take((*st, 0))
                    for t in range(NT):
                        last = nc.tensor.transpose(ps[0:UH, t * P:(t + 1) * P], nmax[:, u % 2, t], ident[:])
                    last.then_inc(made[k], 1)
                elif k == "ST":
                    u, g = st[1:]
                    slot = u % QK_SLOTS
                    if g == 0:
                        pe.wait_ge(m_loaded[u % 2], 32 * (u // 2 + 1))
                    if u == 0 and g == 0:
                        pe.wait_ge(ones_ready, 2)
                    if nth[st]:
                        pe.wait_ge(exp_ready, nth[st])
                    for j in range(GH):
                        h = g * GH + j
                        nc.tensor.matmul(bank(3, 2)[:, j * S:(j + 1) * S], KS[0:SROWS, slot, h, 0:P],
                                         QS[0:SROWS, slot, h, :], start=True, stop=True)
                        last = nc.tensor.matmul(bank(5)[:, j * P:(j + 1) * P], KS[0:SROWS, slot, h, P:S],
                                                QS[0:SROWS, slot, h, P:S], start=True, stop=True)
                    last.then_inc(made[k], 1)
                elif k == "PV":
                    u, g = st[1:]
                    n = u * NG + g
                    pe.wait_ge(masked, n + 1)
                    pe.wait_ge(v_ready, u // 2 + 1)
                    ps = take((*st, 0))
                    for kt in range(NT):
                        for j in range(GH):
                            v = V[:, (u // 2) % V_SLOTS, kt, (u % 2) * UH + g * GH + j]
                            at = j * S if kt == 0 else GH * S + j * P
                            last = nc.tensor.matmul(ps[j * 32:(j + 1) * 32, kt * P:S], v,
                                                    E[:, n % 2, at:at + S - kt * P],
                                                    start=kt == 0, stop=kt == NT - 1, skip_group_check=True)
                    last.then_inc(made[k], 1)
                elif k == "NRM":
                    u = st[1]
                    pe.wait_ge(ou_ready, (u + 1) * NG)
                    ps = take((*st, 0))
                    for g in range(NG):
                        for t in range(NT):
                            c = (g * NT + t) * P
                            last = nc.tensor.transpose(ps[:, c:c + P], OU[:, g, t * P:(t + 1) * P], ident[:])
                    last.then_inc(made[k], 1)
                elif k == "DT":
                    b = st[1]
                    pe.wait_ge(o_ready, (b + 1) * KT)
                    for j in range(2):
                        ps = take((*st, j))
                        for kk in range(2):
                            for t in range(NT):
                                c = (2 * j + kk) * P
                                last = nc.tensor.transpose(ps[:, kk * S + t * P:kk * S + (t + 1) * P],
                                                           XN[:, 2, t, c:c + P], ident[:])
                        last.then_inc(made[k], 1)
                elif k == "WO":
                    b, t = st[1:]
                    if b == 0:
                        pe.wait_ge(wb_hi_ready, 2 * 4)
                        pe.wait_ge(wb_lo_ready, 2 * 4)
                    pe.wait_ge(oh_ready, (b + 1) * 2)
                    pe.wait_ge(ol_ready, (b + 1) * 2)
                    ps = take((*st, 0))
                    for kt in range(KT):
                        last = three_pass(ps, [xt[:, 1, kt, t * P:(t + 1) * P] for xt in (XT_hi, XT_lo)],
                                          [w[:, 3, kt] for w in (wb_hi, wb_lo)], kt == 0, kt == KT - 1)
                    last.then_inc(made[k], 1)


_INS = ["L0_attn_a_x", "L0_attn_a_Wqkv", "L0_attn_a_bqkv", "L0_attn_a_Wo", "L0_attn_a_bo", "L0_attn_b_wq",
        "L0_attn_b_wk", "L0_attn_b_wv", "L0_attn_b_wo", "L0_ffn_qweight", "L0_ffn_scale", "L0_ffn_zero",
        "L0_ffn_bias"]


def kernel(**inputs):
    import concourse.bacc as bacc
    from concourse.bass_utils import run_bass_kernel_spmd

    nc = bacc.Bacc("TRN2", target_bir_lowering=False, num_devices=1)
    arrays = {n: np.ascontiguousarray(inputs[n]) for n in _INS}
    arrays["rope_table"] = rope_tables()
    args = [nc.dram_tensor(n, a.shape, mybir.dt.from_np(a.dtype), kind="ExternalInput").ap()
            for n, a in arrays.items()]
    out = nc.dram_tensor("out", (B, S, C), F32, kind="ExternalOutput").ap()
    hybrid_block_kernel(nc, *args, out)
    r = run_bass_kernel_spmd(nc, [arrays], core_ids=[0])
    return r.results[0]["out"]
```
